# Optimizing a Trainium2 kernel written in Bass

```python
import numpy as np
import jax
import jax.numpy as jnp

def _softmax(x, axis=-1):
    return jax.nn.softmax(x, axis=axis)

def _gelu(x):
    return jax.nn.gelu(x, approximate=True)

def _silu(x):
    return jax.nn.silu(x)

def _sigmoid(x):
    return jax.nn.sigmoid(x)

def _layernorm(x, axis=-1, eps=1e-05):
    m = jnp.mean(x, axis=axis, keepdims=True)
    v = jnp.var(x, axis=axis, keepdims=True)
    return (x - m) / jnp.sqrt(v + eps)

def _scatter_add(tgt, idx, src, axis=0):
    return tgt.at[idx].add(src)

def _segment_sum(src, seg, n):
    return jax.ops.segment_sum(src, seg, n)
kernel_name = 'mk_lm_tower_d1_tok_ids256_r4_c7116a'

def setup_inputs(seed: int=0):
    np.random.seed(seed)
    _w = jnp.asarray

    def _rec_inputs():
        import jax
        import jax.numpy as jnp
        _rk = jax.random.key(seed)
        x = jax.random.randint(jax.random.fold_in(_rk, 1), (64, 128), 0, 1024, jnp.int32)
        return x
    x = _rec_inputs()

    def _L0_tok_setup():
        import jax, jax.numpy as jnp
        import numpy as np
        SEQ_LEN = 1024
        EMB = 64
        BATCH = 4

        def _naive_softmax(s):
            e = jnp.exp(s)
            return e / jnp.sum(e, axis=-1, keepdims=True)
        key = jax.random.key(seed)
        k_x, k_e, k_q, k_k, k_v = jax.random.split(key, 5)
        scale = 0.02
        x = jax.random.randint(k_x, (BATCH, SEQ_LEN), 0, SEQ_LEN)
        emb_table = jax.random.normal(k_e, (SEQ_LEN, EMB), dtype=jnp.float32)
        Wq = jax.random.normal(k_q, (EMB, EMB), dtype=jnp.float32) * scale
        Wk = jax.random.normal(k_k, (EMB, EMB), dtype=jnp.float32) * scale
        Wv = jax.random.normal(k_v, (EMB, EMB), dtype=jnp.float32) * scale
        bq = jnp.zeros((EMB,), dtype=jnp.float32)
        bk = jnp.zeros((EMB,), dtype=jnp.float32)
        bv = jnp.zeros((EMB,), dtype=jnp.float32)
        return {'x': x, 'emb_table': emb_table, 'Wq': Wq, 'bq': bq, 'Wk': Wk, 'bk': bk, 'Wv': Wv, 'bv': bv}
    _L0_tok_all = _L0_tok_setup()
    _L0_tok_in = {k: v for k, v in _L0_tok_all.items() if k in ('emb_table', 'Wq', 'bq', 'Wk', 'bk', 'Wv', 'bv')}
    del _L0_tok_all

    def _L0_attn_setup():
        import math
        import jax, jax.numpy as jnp
        import numpy as np
        EPS_DIV = 1e-07
        EPS_NORM = 1e-12

        def _l2_normalize(x, axis):
            n = jnp.sqrt(jnp.sum(x * x, axis=axis, keepdims=True))
            return x / jnp.maximum(n, EPS_NORM)
        key = jax.random.key(seed)
        ks = jax.random.split(key, 5)
        b, N, C = (8, 1024, 64)
        x = jax.random.normal(ks[0], (b, N, C), dtype=jnp.float32)
        W_qkv = jax.random.normal(ks[1], (C, 3 * C), dtype=jnp.float32) * (1.0 / math.sqrt(C))
        b_qkv = jax.random.normal(ks[2], (3 * C,), dtype=jnp.float32) * 0.02
        W_out = jax.random.normal(ks[3], (C, C), dtype=jnp.float32) * (1.0 / math.sqrt(C))
        b_out = jax.random.normal(ks[4], (C,), dtype=jnp.float32) * 0.02
        return {'x': x, 'W_qkv': W_qkv, 'b_qkv': b_qkv, 'W_out': W_out, 'b_out': b_out}
    _L0_attn_all = _L0_attn_setup()
    _L0_attn_in = {k: v for k, v in _L0_attn_all.items() if k in ('W_qkv', 'b_qkv', 'W_out', 'b_out')}
    del _L0_attn_all

    def _L0_ffn_setup():
        import jax, jax.numpy as jnp
        import numpy as np
        B, S, H, F, E, K = (8, 1024, 64, 128, 16, 2)
        EPS = 1e-05
        key = jax.random.key(seed)
        ks = jax.random.split(key, 9)
        sc = 0.02
        return {'x': jax.random.normal(ks[0], (B, S, H), dtype=jnp.float32), 'gate_w': jax.random.normal(ks[1], (H, E), dtype=jnp.float32) * sc, 'gate_b': jnp.zeros((E,), dtype=jnp.float32), 'w1': jax.random.normal(ks[2], (E, H, F), dtype=jnp.float32) * sc, 'b1': jnp.zeros((E, F), dtype=jnp.float32), 'w2': jax.random.normal(ks[3], (E, F, H), dtype=jnp.float32) * sc, 'b2': jnp.zeros((E, H), dtype=jnp.float32), 'gamma': jnp.ones((H,), dtype=jnp.float32), 'beta': jnp.zeros((H,), dtype=jnp.float32)}
    _L0_ffn_all = _L0_ffn_setup()
    _L0_ffn_in = {k: v for k, v in _L0_ffn_all.items() if k in ('gate_w', 'gate_b', 'w1', 'b1', 'w2', 'b2', 'gamma', 'beta')}
    del _L0_ffn_all
    return {'x': x, 'L0_tok_emb_table': _L0_tok_in['emb_table'], 'L0_tok_Wq': _L0_tok_in['Wq'], 'L0_tok_bq': _L0_tok_in['bq'], 'L0_tok_Wk': _L0_tok_in['Wk'], 'L0_tok_bk': _L0_tok_in['bk'], 'L0_tok_Wv': _L0_tok_in['Wv'], 'L0_tok_bv': _L0_tok_in['bv'], 'L0_attn_W_qkv': _L0_attn_in['W_qkv'], 'L0_attn_b_qkv': _L0_attn_in['b_qkv'], 'L0_attn_W_out': _L0_attn_in['W_out'], 'L0_attn_b_out': _L0_attn_in['b_out'], 'L0_ffn_gate_w': _L0_ffn_in['gate_w'], 'L0_ffn_gate_b': _L0_ffn_in['gate_b'], 'L0_ffn_w1': _L0_ffn_in['w1'], 'L0_ffn_b1': _L0_ffn_in['b1'], 'L0_ffn_w2': _L0_ffn_in['w2'], 'L0_ffn_b2': _L0_ffn_in['b2'], 'L0_ffn_gamma': _L0_ffn_in['gamma'], 'L0_ffn_beta': _L0_ffn_in['beta']}

def reference(x, L0_tok_emb_table, L0_tok_Wq, L0_tok_bq, L0_tok_Wk, L0_tok_bk, L0_tok_Wv, L0_tok_bv, L0_attn_W_qkv, L0_attn_b_qkv, L0_attn_W_out, L0_attn_b_out, L0_ffn_gate_w, L0_ffn_gate_b, L0_ffn_w1, L0_ffn_b1, L0_ffn_w2, L0_ffn_b2, L0_ffn_gamma, L0_ffn_beta):
    import jax
    import jax.numpy as jnp

    def _L0_tok_ref(x, emb_table, Wq, bq, Wk, bk, Wv, bv):
        import jax, jax.numpy as jnp
        import numpy as np
        SEQ_LEN = 1024
        EMB = 64
        BATCH = 4

        def _naive_softmax(s):
            e = jnp.exp(s)
            return e / jnp.sum(e, axis=-1, keepdims=True)
        emb = emb_table[x]
        q = emb @ Wq + bq
        k = emb @ Wk + bk
        v = emb @ Wv + bv
        inv = 1.0 / jnp.sqrt(jnp.float32(EMB))
        score = jnp.einsum('bse,bte->bst', q, k) * inv
        attn = _naive_softmax(score)
        return jnp.einsum('bst,bte->bse', attn, v)

    def _L0_attn_ref(x, W_qkv, b_qkv, W_out, b_out):
        import math
        import jax, jax.numpy as jnp
        import numpy as np
        EPS_DIV = 1e-07
        EPS_NORM = 1e-12

        def _l2_normalize(x, axis):
            n = jnp.sqrt(jnp.sum(x * x, axis=axis, keepdims=True))
            return x / jnp.maximum(n, EPS_NORM)
        b, N, C = x.shape
        qkv = x @ W_qkv + b_qkv
        q, k, v = jnp.split(qkv, 3, axis=2)
        q = q - jnp.mean(q, axis=2, keepdims=True)
        k = k - jnp.mean(k, axis=2, keepdims=True)
        q2 = q * q
        k2 = k * k
        q2s = jnp.sum(q2, axis=2, keepdims=True)
        k2s = jnp.sum(k2, axis=2, keepdims=True)
        k2 = _l2_normalize(k2 / (k2s + EPS_DIV), axis=-2)
        q2 = _l2_normalize(q2 / (q2s + EPS_DIV), axis=-1)
        kv = jnp.einsum('bnc,bnd->bcd', k2, v)
        t2 = jnp.einsum('bnc,bcd->bnd', q2, kv) / math.sqrt(N)
        attn = v + t2
        return attn @ W_out + b_out

    def _L0_ffn_ref(x, gate_w, gate_b, w1, b1, w2, b2, gamma, beta):
        import jax, jax.numpy as jnp
        import numpy as np
        B, S, H, F, E, K = (8, 1024, 64, 128, 16, 2)
        EPS = 1e-05
        gate_logits = x @ gate_w + gate_b
        topk_vals, topk_idx = jax.lax.top_k(gate_logits, K)
        topk_w = jax.nn.softmax(topk_vals, axis=-1)
        h = jax.nn.relu(jnp.einsum('bsh,ehf->bsef', x, w1) + b1)
        expert_out = jnp.einsum('bsef,efh->bseh', h, w2) + b2
        sel = jnp.take_along_axis(expert_out, topk_idx[:, :, :, None], axis=2)
        moe = jnp.sum(topk_w[..., None] * sel, axis=2)
        y = x + moe
        mu = jnp.mean(y, axis=-1, keepdims=True)
        var = jnp.var(y, axis=-1, keepdims=True)
        return (y - mu) / jnp.sqrt(var + EPS) * gamma + beta
    h = _L0_tok_ref(x, L0_tok_emb_table, L0_tok_Wq, L0_tok_bq, L0_tok_Wk, L0_tok_bk, L0_tok_Wv, L0_tok_bv)
    h = h + _L0_attn_ref(_layernorm(h, axis=-1), L0_attn_W_qkv, L0_attn_b_qkv, L0_attn_W_out, L0_attn_b_out)
    h = h + _L0_ffn_ref(_layernorm(h, axis=-1), L0_ffn_gate_w, L0_ffn_gate_b, L0_ffn_w1, L0_ffn_b1, L0_ffn_w2, L0_ffn_b2, L0_ffn_gamma, L0_ffn_beta)
    return h

_drawn_inputs = setup_inputs


def setup_inputs(seed=0):
    import zlib

    import numpy as np

    out = dict(_drawn_inputs(seed))
    spreads = {'L0_tok_bq': (0.0, 0.8),
     'L0_tok_bk': (0.0, 0.8),
     'L0_tok_bv': (0.0, 0.1),
     'L0_ffn_gate_b': (0.0, 0.786),
     'L0_ffn_b1': (0.0, 0.8),
     'L0_ffn_b2': (0.0, 0.8),
     'L0_ffn_gamma': (1.0, 0.2),
     'L0_ffn_beta': (0.0, 0.516)}
    factors = {'L0_tok_Wq': 8.0,
     'L0_tok_Wk': 8.0,
     'L0_attn_b_qkv': 2.976,
     'L0_attn_b_out': 8.0,
     'L0_ffn_gate_w': 5.505,
     'L0_ffn_w1': 8.0,
     'L0_ffn_w2': 8.0}
    for name, (base, spread) in spreads.items():
        noise = np.random.default_rng([zlib.crc32(name.encode()), seed]).standard_normal(out[name].shape)
        drawn = base * np.exp(spread * noise) if base else spread * noise
        out[name] = jnp.asarray(drawn.astype(out[name].dtype))
    for name, factor in factors.items():
        out[name] = (out[name] * factor).astype(out[name].dtype)
    return out
```

```python
from contextlib import ExitStack

import concourse.bass as bass
from concourse import mybir

F32 = mybir.dt.float32
F32R = mybir.dt.float32r
I32 = mybir.dt.int32
U32 = mybir.dt.uint32
ACT = mybir.ActivationFunctionType
ALU = mybir.AluOpType
AX = mybir.AxisListType

P = 128
CHUNK = 4
PAIRS = CHUNK // 2
SLOTS = 8
Z_BANKS = 3
RING = 4
LN_EPS = 1e-5
SUM_EPS = 1e-7
NORM_EPS = 1e-12


class Chunk:

    def __init__(self, number, half, parity):
        self.number, self.half, self.parity = number, half, parity

    def at(self, per_chunk, n):
        return self.number * per_chunk + n

    def before(self, per_chunk, n=None):
        if isinstance(self.number, int) and self.number == 0:
            return None
        return (self.number - 1) * per_chunk + (per_chunk if n is None else n)


class Step:

    def __init__(self, k, chunks, m=None):
        def chunk(off):
            n = k + off
            if m is not None:
                return Chunk(2 * m + n, m + n // 2, n % 2)
            return Chunk(n, n // 2, n % 2) if 0 <= n < chunks else None

        self.old, self.moe, self.mid, self.new, self.fetch = (chunk(o) for o in (-1, 0, 1, 2, 3))


def steps(engine, chunks, body):
    first, last = 2, (chunks - 3) // 2 * 2
    for k in range(-3, first):
        body(Step(k, chunks))
    with engine.Fori(first // 2, last // 2) as m:
        body(Step(0, chunks, m))
        body(Step(1, chunks, m))
    for k in range(last, chunks + 1):
        body(Step(k, chunks))


def wait(engine, semaphore, value):
    if value is not None:
        engine.wait_ge(semaphore, value)


def build(nc, x, emb, Wq, bq, Wk, bk, Wv, bv, W_qkv, b_qkv, W_out, b_out,
          gate_w, gate_b, w1, b1, w2, b2, gamma, beta, out):
    SEQS, T = x.shape
    VOCAB, C = emb.shape
    E, _, F = w1.shape
    CHUNKS = SEQS // CHUNK
    TOK = CHUNK * T
    VT = VOCAB // P
    GW = 200
    assert T == P and F == P and C == 64 and E == 2 * SLOTS and CHUNKS % 2 == 0
    SCORE_SCALE = float(C) ** -0.5
    KV_SCALE = float(T) ** -0.5

    table = nc.dram_tensor("qkv_table", (VOCAB, 3 * C), F32, kind="Internal").ap()

    with ExitStack() as ctx:
        def sb(name, shape, dt=F32):
            return ctx.enter_context(nc.sbuf_tensor(name, shape, dt))

        def ps(name):
            return ctx.enter_context(nc.psum_tensor(name, [P, 512], F32))

        def sem(name):
            return ctx.enter_context(nc.semaphore(name))

        bank_a, bank_b, bank_c, bank_d, bank_acc = (ps(n) for n in ("bank_a", "bank_b", "bank_c", "bank_d", "bank_acc"))
        bank_z = [ps(f"bank_z{i}") for i in range(Z_BANKS)]

        ident = sb("ident", [P, P])
        ident2 = sb("ident2", [P, C])
        iota = sb("iota", [P, E])
        iota_i = sb("iota_i", [P, E], I32)
        minus_half = sb("minus_half", [P, 2 * CHUNK])
        tok_w = sb("tok_w", [C + 1, 3 * C])
        qkv_w = sb("qkv_w", [C + 1, 3 * C])
        wout = sb("wout", [C, C])
        wv_t = sb("wv_t", [C, C + 1])
        qk_mean = sb("qk_mean", [C + 1, 2])
        gate_raw = sb("gate_raw", [P, E])
        gate_hi = sb("gate_hi", [P, E], F32R)
        gate_lo = sb("gate_lo", [P, E], F32R)
        gate_bias = sb("gate_bias", [P, E])
        w1_raw = sb("w1_raw", [P, E * F])
        w1_hi = sb("w1_hi", [P, E * F], F32R)
        w1_lo = sb("w1_lo", [P, E * F], F32R)
        w2_s = sb("w2_s", [P, E, C])
        b1_s = sb("b1_s", [E, F])
        b1_neg = sb("b1_neg", [P, E])
        b1_diag = sb("b1_diag", [P, E, E])
        b2_s = sb("b2_s", [E, C])
        gate_const = sb("gate_const", [E, C])
        out_bias = sb("out_bias", [P, C])
        gamma_s = sb("gamma_s", [P, C])
        beta_s = sb("beta_s", [P, C])
        emb_s = sb("emb_s", [P, VT, C])
        emb_t = sb("emb_t", [C + 1, VOCAB])
        table_s = sb("table_s", [P, VT, 3 * C])
        x_s = sb("x_s", [SEQS, T], I32)
        x_f = sb("x_f", [SEQS, T])
        tok_id = sb("tok_id", [P, SEQS], I32)
        rows_now = [sb(f"rows_now{i}", [P, CHUNK], I32) for i in range(2)]
        gath = [sb(f"gath{i}", [P, CHUNK, GW]) for i in range(2)]
        qk_t = sb("qk_t", [P, 2, PAIRS, P])
        probs = sb("probs", [P, CHUNK, P])
        rsum = sb("rsum", [P, CHUNK])
        h1 = sb("h1", [P, CHUNK, C])
        h1b = [sb(f"h1b{i}", [P, CHUNK, C]) for i in range(2)]
        stats = [sb(f"stats{i}", [P, CHUNK, 6]) for i in range(3)]
        mv = [sb(f"mv{i}", [P, CHUNK, 2]) for i in range(3)]
        rstd = [sb(f"rstd{i}", [P, CHUNK]) for i in range(3)]
        var = [sb(f"var{i}", [P, CHUNK]) for i in range(3)]
        x1 = sb("x1", [P, CHUNK, C + 1])
        x1_t = sb("x1_t", [C + 1, TOK])
        sq = sb("sq", [P, CHUNK, 2 * C])
        sq_sum = sb("sq_sum", [P, 2 * CHUNK])
        sq_rec = sb("sq_rec", [P, 2 * CHUNK])
        qkv2 = sb("qkv2", [P, CHUNK, 3 * C])
        q4 = sb("q4", [P, CHUNK, C])
        q4_sum = sb("q4_sum", [P, CHUNK])
        q4_max = sb("q4_max", [P, CHUNK])
        q_rn = sb("q_rn", [P, CHUNK])
        q2n = sb("q2n", [P, PAIRS, 2, C])
        q2n_t = sb("q2n_t", [P, PAIRS, P])
        gram = sb("gram", [P, PAIRS, C])
        k_sum = sb("k_sum", [P, PAIRS])
        k_max = sb("k_max", [P, PAIRS])
        k_rn = sb("k_rn", [P, PAIRS])
        kv = sb("kv", [P, PAIRS, C])
        h2 = [sb(f"h2{i}", [P, CHUNK, C]) for i in range(2)]
        x3 = [sb(f"x3{i}", [P, CHUNK, 2, C]) for i in range(2)]
        x3_t = [sb(f"x3_t{i}", [P, TOK], F32R) for i in range(2)]
        logits = sb("logits", [P, CHUNK, E])
        top = sb("top", [P, CHUNK, 8])
        top_at = sb("top_at", [P, CHUNK, 8], U32)
        gap = sb("gap", [P, CHUNK])
        gap_exp = sb("gap_exp", [P, CHUNK])
        gap_sum = sb("gap_sum", [P, CHUNK])
        top_w = sb("top_w", [P, CHUNK, 2])
        chosen = sb("chosen", [P, CHUNK, 2, E])
        weighed = sb("weighed", [P, CHUNK, 2, E])
        gates = sb("gates", [P, CHUNK, E])
        gates_t = [sb(f"gates_t{i}", [E, TOK]) for i in range(2)]
        gates_row = [sb(f"gates_row{i}", [1, E * TOK]) for i in range(2)]
        spread = [sb(f"spread{i}", [P, TOK]) for i in range(RING)]
        hidden = [sb(f"hidden{i}", [P, TOK]) for i in range(RING)]
        moe_t = sb("moe_t", [P, TOK])
        y = sb("y", [P, CHUNK, C])
        yn = sb("yn", [P, CHUNK, C])
        yg = sb("yg", [P, CHUNK, C])
        h2b = sb("h2b", [P, CHUNK, C])
        res = sb("res", [P, CHUNK, C])

        x_in = sem("x_in")
        emb_in = sem("emb_in")
        tokw_in = sem("tokw_in")
        small_in = sem("small_in")
        w1_in = sem("w1_in")
        const_set = sem("const_set")
        ones_set = sem("ones_set")
        setup_pe = sem("setup_pe")
        setup_dve = sem("setup_dve")
        emb_t_set = sem("emb_t_set")
        table_mm = sem("table_mm")
        table_ev = sem("table_ev")
        table_out = sem("table_out")
        gathered = [sem(f"gathered{i}") for i in range(2)]
        qk_turned = sem("qk_turned")
        scored = sem("scored")
        pv_done = sem("pv_done")
        x1_turned = sem("x1_turned")
        qkv_done = sem("qkv_done")
        kv_done = sem("kv_done")
        q_turned = sem("q_turned")
        t2_done = sem("t2_done")
        x3_turned = sem("x3_turned")
        logits_done = sem("logits_done")
        gates_turned = sem("gates_turned")
        z_ready = sem("z_ready")
        hidden_used = sem("hidden_used")
        moe_done = sem("moe_done")
        qk_copied = sem("qk_copied")
        exp_done = sem("exp_done")
        x1_copied = sem("x1_copied")
        squared = sem("squared")
        v_copied = sem("v_copied")
        q4_done = sem("q4_done")
        q_copied = sem("q_copied")
        x3_high = sem("x3_high")
        gap_done = sem("gap_done")
        gates_copied = sem("gates_copied")
        acc_copied = sem("acc_copied")
        ln_stat = [sem(f"ln_stat{i}") for i in range(3)]
        x1_step = sem("x1_step")
        q_step = sem("q_step")
        k_step = sem("k_step")
        h2_done = sem("h2_done")
        x3_done = sem("x3_done")
        x3_low = sem("x3_low")
        gate_step = sem("gate_step")
        hidden_ready = sem("hidden_ready")
        y_done = sem("y_done")
        yn_done = sem("yn_done")
        res_done = sem("res_done")
        ln_pool = [sem(f"ln_pool{i}") for i in range(3)]
        q_pool = sem("q_pool")
        k_pool = sem("k_pool")
        h1b_done = sem("h1b_done")
        h2b_done = sem("h2b_done")
        yg_done = sem("yg_done")
        spread_done = sem("spread_done")
        rows_set = sem("rows_set")
        row_in = [sem(f"row_in{i}") for i in range(2)]
        stored = sem("stored")

        N_X1, N_Q, N_K, N_GATE = 3, 6, 3, 7 + 2 * CHUNK

        def fixed(engine):
            engine.nop(nofuse=True)

        block = ctx.enter_context(nc.Block())

        @block.sync
        def _(sp):
            sp.dma_start(x_s[:], x).then_inc(x_in, 16)
            sp.dma_start(emb_s[:], emb.rearrange("(t p) c -> p t c", p=P)).then_inc(emb_in, 16)
            for i, (w, b) in enumerate(((Wq, bq), (Wk, bk), (Wv, bv))):
                sp.dma_start(tok_w[0:C, i * C:(i + 1) * C], w).then_inc(tokw_in, 16)
                sp.dma_start(tok_w[C:C + 1, i * C:(i + 1) * C], b.rearrange("(a c) -> a c", a=1)).then_inc(tokw_in, 16)
            sp.dma_start(qkv_w[0:C, :], W_qkv).then_inc(small_in, 16)
            sp.dma_start(qkv_w[C:C + 1, :], b_qkv.rearrange("(a c) -> a c", a=1)).then_inc(small_in, 16)
            sp.dma_start(wout[:], W_out).then_inc(small_in, 16)
            sp.dma_start(out_bias[:], b_out.partition_broadcast(P)).then_inc(small_in, 16)
            sp.dma_start(b1_s[:], b1).then_inc(small_in, 16)
            sp.dma_start(b2_s[:], b2).then_inc(small_in, 16)
            sp.dma_start(w2_s[:], w2.rearrange("e f c -> f e c")).then_inc(small_in, 16)
            for half in range(2):
                sp.dma_start(gate_raw[half * C:(half + 1) * C, :], gate_w).then_inc(small_in, 16)
                sp.dma_start(w1_raw[half * C:(half + 1) * C, :].rearrange("c (e f) -> c e f", e=E),
                             w1.rearrange("e c f -> c e f")).then_inc(w1_in, 16)
            sp.dma_start(gate_bias[:], gate_b.partition_broadcast(P)).then_inc(small_in, 16)
            sp.dma_start(gamma_s[:], gamma.partition_broadcast(P)).then_inc(small_in, 16)
            sp.dma_start(beta_s[:], beta.partition_broadcast(P)).then_inc(small_in, 16)
            sp.wait_ge(table_ev, VT)
            sp.dma_start(table.rearrange("(t p) c -> p t c", p=P), table_s[:]).then_inc(table_out, 16)

            def body(st):
                if st.mid:
                    c = st.mid
                    sp.wait_ge(gates_copied, c.at(1, 1))
                    fixed(sp)
                    if not (isinstance(c.number, int) and c.number < 2):
                        sp.wait_ge(spread_done, (c.number - 1) * E)
                    sp.dma_start(gates_row[c.parity][:].rearrange("a (e t) -> a e t", e=E),
                                 gates_t[c.parity][:]).then_inc(row_in[c.parity], 16)
                if st.old:
                    c = st.old
                    sp.wait_ge(res_done, c.at(1, 1))
                    fixed(sp)
                    rows = out[bass.ds(c.number * CHUNK, CHUNK), :, :].rearrange("s t c -> t s c")
                    sp.dma_start(rows, res[:]).then_inc(stored, 16)

            steps(sp, CHUNKS, body)
            sp.wait_ge(stored, 16 * CHUNKS)

        @block.gpsimd
        def _(pool):
            nc.gpsimd.memset(ident[:], 0.0).then_inc(const_set, 1)
            nc.gpsimd.memset(ident2[:], 0.0).then_inc(const_set, 1)
            nc.gpsimd.memset(minus_half[:], -0.5).then_inc(const_set, 1)
            nc.gpsimd.iota(iota_i[:], pattern=[[1, E]], base=0, channel_multiplier=0).then_inc(const_set, 1)
            pool.wait_ge(const_set, 4)
            nc.gpsimd.affine_select(out=ident[:], in_=ident[:], compare_op=ALU.not_equal, fill=1.0, base=0,
                                    pattern=[[-1, P]], channel_multiplier=1).then_inc(const_set, 1)
            nc.gpsimd.affine_select(out=ident2[:], in_=ident2[:], compare_op=ALU.not_equal, fill=1.0, base=0,
                                    pattern=[[-1, C]], channel_multiplier=1).then_inc(const_set, 1)
            pool.wait_ge(const_set, 6)
            nc.gpsimd.affine_select(out=ident2[:], in_=ident2[:], compare_op=ALU.not_equal, fill=1.0, base=-C,
                                    pattern=[[-1, C]], channel_multiplier=1).then_inc(const_set, 1)
            nc.gpsimd.tensor_copy(iota[:], iota_i[:]).then_inc(const_set, 1)
            nc.gpsimd.memset(b1_diag[:], 0.0).then_inc(const_set, 1)
            nc.gpsimd.memset(x1[:, :, C:C + 1], 1.0).then_inc(ones_set, 1)
            nc.gpsimd.memset(gath[0][:, :, 3 * C:3 * C + 1], 1.0).then_inc(ones_set, 1)
            nc.gpsimd.memset(gath[1][:, :, 3 * C:3 * C + 1], 1.0).then_inc(ones_set, 1)
            pool.wait_ge(small_in, 16 * 12)
            pool.wait_ge(table_out, 16)
            pool.wait_ge(setup_dve, 5)

            def inverse_root(i, c):
                pool.wait_ge(ln_stat[i], c.at(2 * CHUNK, 2 * CHUNK))
                fixed(pool)
                nc.gpsimd.tensor_scalar(var[i][:], mv[i][:, :, 1], LN_EPS, None, ALU.add).then_inc(ln_pool[i], 1)
                pool.wait_ge(ln_pool[i], c.at(2, 1))
                nc.gpsimd.tensor_tensor(rstd[i][:], var[i][:], minus_half[:, 0:CHUNK], ALU.pow).then_inc(ln_pool[i], 1)

            def broadcast(c, e):
                if e == 0:
                    pool.wait_ge(row_in[c.parity], 16 * (c.half + 1))
                if e >= RING or c.before(E) is not None:
                    pool.wait_ge(hidden_ready, c.at(E, e - RING + 1))
                fixed(pool)
                nc.gpsimd.partition_broadcast(spread[e % RING][:], gates_row[c.parity][0:1, e * TOK:(e + 1) * TOK],
                                              channels=P).then_inc(spread_done, 1)

            def body(st):
                for j in range(SLOTS):
                    if j < SLOTS - 1:
                        if st.moe:
                            broadcast(st.moe, 2 * j + 2)
                            broadcast(st.moe, 2 * j + 3)
                    elif st.mid:
                        broadcast(st.mid, 0)
                        broadcast(st.mid, 1)
                    if j == 0 and st.mid:
                        inverse_root(1, st.mid)
                    if j == 0 and st.old:
                        inverse_root(2, st.old)
                    if j == 1 and st.old:
                        c = st.old
                        pool.wait_ge(yn_done, c.at(CHUNK, CHUNK))
                        wait(pool, res_done, c.before(1))
                        nc.gpsimd.tensor_tensor(yg[:], yn[:], gamma_s[:].unsqueeze(1).to_broadcast([P, CHUNK, C]),
                                                ALU.mult).then_inc(yg_done, 1)
                    if j == 3 and st.new:
                        c = st.new
                        inverse_root(0, c)
                    if j == 4 and st.new:
                        c = st.new
                        pool.wait_ge(x1_step, c.at(N_X1, 2))
                        nc.gpsimd.tensor_tensor(h1b[c.parity][:], h1[:],
                                                out_bias[:].unsqueeze(1).to_broadcast([P, CHUNK, C]),
                                                ALU.add).then_inc(h1b_done, 1)
                    if j == 4 and st.fetch:
                        c = st.fetch
                        if not (isinstance(c.number, int) and c.number < 2):
                            pool.wait_ge(pv_done, c.number - 1)
                            pool.wait_ge(gathered[c.parity], 16 * CHUNK * c.half)
                        nc.gpsimd.tensor_copy(rows_now[c.parity][:], tok_id[:, bass.ds(c.number * CHUNK, CHUNK)])\
                          .then_inc(rows_set, 1)
                        pool.wait_ge(rows_set, c.at(1, 1))
                        fixed(pool)
                        for s in range(CHUNK):
                            nc.gpsimd.indirect_dma_start(
                                gath[c.parity][:, s, 0:3 * C], None, table,
                                bass.IndirectOffsetOnAxis(ap=rows_now[c.parity][:, s:s + 1], axis=0),
                            ).then_inc(gathered[c.parity], 16)
                    if j == 5 and st.new:
                        c = st.new
                        pool.wait_ge(q_step, c.at(N_Q, 5))
                        fixed(pool)
                        nc.gpsimd.tensor_scalar(q4_max[:], q4_sum[:], NORM_EPS ** 2, None, ALU.max).then_inc(q_pool, 1)
                        pool.wait_ge(q_pool, c.at(2, 1))
                        nc.gpsimd.tensor_tensor(q_rn[:], q4_max[:], minus_half[:, 0:CHUNK], ALU.pow).then_inc(q_pool, 1)
                    if j == 5 and st.moe:
                        c = st.moe
                        pool.wait_ge(h2_done, c.at(2, 2))
                        wait(pool, res_done, c.before(1))
                        nc.gpsimd.tensor_tensor(h2b[:], h2[c.parity][:],
                                                beta_s[:].unsqueeze(1).to_broadcast([P, CHUNK, C]),
                                                ALU.add).then_inc(h2b_done, 1)
                    if j == 6 and st.new:
                        c = st.new
                        pool.wait_ge(k_step, c.at(N_K, 2))
                        fixed(pool)
                        nc.gpsimd.tensor_scalar(k_max[:], k_sum[:], NORM_EPS ** 2, None, ALU.max).then_inc(k_pool, 1)
                        pool.wait_ge(k_pool, c.at(2, 1))
                        nc.gpsimd.tensor_tensor(k_rn[:], k_max[:], minus_half[:, 0:PAIRS], ALU.pow).then_inc(k_pool, 1)

            steps(pool, CHUNKS, body)

        @block.scalar
        def _(act):
            for t in range(VT):
                act.wait_ge(table_mm, t + 1)
                nc.scalar.copy(table_s[:, t, :], (bank_b if t % 2 == 0 else bank_c)[:, 0:3 * C]).then_inc(table_ev, 1)

            def body(st):
                if st.old:
                    c = st.old
                    act.wait_ge(hidden_used, c.at(E, E))
                    wait(act, moe_done, c.before(1))
                    nc.scalar.copy(moe_t[:], bank_acc[:]).then_inc(acc_copied, 1)
                if st.mid:
                    c = st.mid
                    act.wait_ge(x3_turned, c.at(1, 1))
                    if not (isinstance(c.number, int) and c.number < 2):
                        act.wait_ge(hidden_used, (c.number - 1) * E)
                    nc.scalar.copy(x3_t[c.parity][:], bank_d[:]).then_inc(x3_high, 1)
                if st.new:
                    c = st.new
                    act.wait_ge(qk_turned, c.at(1, 1))
                    wait(act, scored, c.before(1))
                    for half in range(2):
                        rows = slice(half * C, (half + 1) * C)
                        cols = slice(half * PAIRS * P, (half + 1) * PAIRS * P)
                        for i in range(2):
                            nc.scalar.copy(qk_t[rows, i, :, :].rearrange("p a t -> p (a t)"),
                                           bank_a[i * C:(i + 1) * C, cols]).then_inc(qk_copied, 1)
                    act.wait_ge(scored, c.at(1, 1))
                    wait(act, pv_done, c.before(1))
                    for half, bank in ((0, bank_b), (1, bank_c)):
                        nc.scalar.activation(probs[:, 2 * half:2 * half + 2, :].rearrange("p s t -> p (s t)"),
                                             bank[:, 0:2 * P], ACT.Exp, scale=SCORE_SCALE).then_inc(exp_done, 1)
                if st.mid:
                    c = st.mid
                    act.wait_ge(gate_step, c.at(N_GATE, 2 + 2 * CHUNK))
                    nc.scalar.activation(gap_exp[:], gap[:], ACT.Exp).then_inc(gap_done, 1)
                    act.wait_ge(gates_turned, c.at(1, 1))
                    if not (isinstance(c.number, int) and c.number < 2):
                        act.wait_ge(row_in[c.parity], 16 * c.half)
                        act.wait_ge(hidden_used, (c.number - 1) * E)
                    nc.scalar.copy(gates_t[c.parity][:], bank_d[0:E, :]).then_inc(gates_copied, 1)
                if st.new:
                    c = st.new
                    act.wait_ge(x1_turned, c.at(1, 1))
                    wait(act, qkv_done, c.before(1))
                    nc.scalar.copy(x1_t[:], bank_a[0:C + 1, :]).then_inc(x1_copied, 1)
                    act.wait_ge(qkv_done, c.at(1, 1))
                    wait(act, q_step, c.before(N_Q, 4))
                    wait(act, kv_done, c.before(1))
                    for half, bank in ((0, bank_b), (1, bank_c)):
                        both = bank[:, 0:2 * 3 * C].rearrange("p (s n) -> p s n", s=2)
                        nc.scalar.activation(sq[:, 2 * half:2 * half + 2, :], both[:, :, 0:2 * C], ACT.Square)\
                          .then_inc(squared, 1)
                        nc.scalar.copy(qkv2[:, 2 * half:2 * half + 2, 2 * C:3 * C], both[:, :, 2 * C:3 * C])\
                          .then_inc(v_copied, 1)
                    act.wait_ge(q_step, c.at(N_Q, 4))
                    nc.scalar.activation(q4[:], qkv2[:, :, 0:C], ACT.Square).then_inc(q4_done, 1)
                    act.wait_ge(q_turned, c.at(1, 1))
                    wait(act, t2_done, c.before(1))
                    nc.scalar.copy(q2n_t[:].rearrange("p a t -> p (a t)"), bank_d[:, 0:2 * P]).then_inc(q_copied, 1)

            steps(act, CHUNKS, body)

        @block.vector
        def _(dve):
            dve.wait_ge(x_in, 16)
            nc.vector.tensor_copy(x_f[:], x_s[:]).then_inc(setup_dve, 1)
            dve.wait_ge(w1_in, 32)
            nc.vector.tensor_copy(w1_hi[:], w1_raw[:]).then_inc(setup_dve, 1)
            dve.wait_ge(setup_dve, 2)
            nc.vector.tensor_tensor(w1_lo[:], w1_raw[:], w1_hi[:].bitcast(F32), ALU.subtract).then_inc(setup_dve, 1)
            nc.vector.memset(emb_t[C:C + 1, :], 1.0).then_inc(setup_dve, 1)
            dve.wait_ge(setup_pe, 1)
            nc.vector.tensor_copy(tok_id[:], bank_d[:, 0:SEQS]).then_inc(setup_dve, 1)
            for half in range(2):
                dve.wait_ge(setup_pe, 2 + half)
                nc.vector.tensor_copy(emb_t[0:C, half * 512:(half + 1) * 512],
                                      (bank_a if half == 0 else bank_acc)[0:C, :]).then_inc(emb_t_set, 1)
            dve.wait_ge(small_in, 16 * 12)
            nc.vector.tensor_reduce(qk_mean[:], qkv_w[:, 0:2 * C].rearrange("p (a c) -> p a c", a=2), AX.X, ALU.add)\
              .then_inc(setup_dve, 1)
            dve.wait_ge(setup_dve, 6)
            nc.vector.tensor_scalar(qk_mean[:], qk_mean[:], 1.0 / C, None, ALU.mult).then_inc(setup_dve, 1)
            dve.wait_ge(setup_dve, 7)
            for i in range(2):
                nc.vector.tensor_scalar(qkv_w[:, i * C:(i + 1) * C], qkv_w[:, i * C:(i + 1) * C],
                                        qk_mean[:, i:i + 1], None, ALU.subtract).then_inc(setup_dve, 1)
            nc.vector.tensor_copy(gate_hi[:], gate_raw[:]).then_inc(setup_dve, 1)
            dve.wait_ge(setup_dve, 10)
            nc.vector.tensor_tensor(gate_lo[:], gate_raw[:], gate_hi[:].bitcast(F32), ALU.subtract)\
              .then_inc(setup_dve, 1)
            dve.wait_ge(setup_pe, 4)
            nc.vector.tensor_copy(wv_t[:], bank_z[0][0:C, 0:C + 1]).then_inc(setup_dve, 1)
            nc.vector.tensor_scalar(b1_neg[:], bank_z[0][:, 128:128 + E], -1.0, None, ALU.mult).then_inc(setup_dve, 1)
            dve.wait_ge(const_set, 9)
            nc.vector.tensor_copy(b1_diag[:].rearrange("p a b -> p (a b)")[:, 0:E * E:E + 1],
                                  bank_z[0][:, 128:128 + E]).then_inc(setup_dve, 1)
            dve.wait_ge(setup_pe, 5)
            nc.vector.tensor_copy(qkv_w[:, 2 * C:3 * C], bank_z[1][0:C + 1, 0:C]).then_inc(setup_dve, 1)
            dve.wait_ge(setup_pe, 6)
            nc.vector.tensor_tensor(gate_const[:], bank_z[2][0:E, 0:C], b2_s[:], ALU.add).then_inc(setup_dve, 1)

            def ln_stats(i, c, src):
                for s in range(CHUNK):
                    nc.vector.bn_stats(stats[i][:, s, :], src[:, s, :]).then_inc(ln_stat[i], 1)
                dve.wait_ge(ln_stat[i], c.at(2 * CHUNK, CHUNK))
                fixed(dve)
                for s in range(CHUNK):
                    nc.vector.bn_aggr(mv[i][:, s, :], stats[i][:, s, :]).then_inc(ln_stat[i], 1)

            def expert(c, e):
                dve.wait_ge(z_ready, c.at(E, e + 1))
                dve.wait_ge(spread_done, c.at(E, e + 1))
                if e >= RING or c.before(E) is not None:
                    dve.wait_ge(hidden_used, c.at(E, e - RING + 1))
                nc.vector.scalar_tensor_tensor(hidden[e % RING][:], bank_z[e % Z_BANKS][:], b1_neg[:, e:e + 1],
                                               spread[e % RING][:], ALU.max, ALU.mult).then_inc(hidden_ready, 1)

            def body(st):
                for j in range(SLOTS):
                    if st.moe:
                        expert(st.moe, 2 * j)
                        expert(st.moe, 2 * j + 1)
                    if j == 0 and st.mid:
                        c = st.mid
                        dve.wait_ge(t2_done, c.at(1, 1))
                        dve.wait_ge(h1b_done, c.at(1, 1))
                        if not (isinstance(c.number, int) and c.number < 2):
                            dve.wait_ge(h2b_done, c.number - 1)
                        for half, bank in ((0, bank_b), (1, bank_c)):
                            v_part = bank[:, 0:2 * 3 * C].rearrange("p (s n) -> p s n", s=2)[:, :, 2 * C:3 * C]
                            nc.vector.tensor_tensor(h2[c.parity][:, 2 * half:2 * half + 2, :], v_part,
                                                    h1b[c.parity][:, 2 * half:2 * half + 2, :], ALU.add)\
                              .then_inc(h2_done, 1)
                        dve.wait_ge(h2_done, c.at(2, 2))
                        wait(dve, ln_pool[1], c.before(2))
                        ln_stats(1, c, h2[c.parity])
                    if j == 0 and st.old:
                        c = st.old
                        dve.wait_ge(moe_done, c.at(1, 1))
                        nc.vector.tensor_tensor(y[:], bank_a[:, 0:CHUNK * C].rearrange("p (s c) -> p s c", s=CHUNK),
                                                x3[c.parity][:, :, 0, :], ALU.add).then_inc(y_done, 1)
                        dve.wait_ge(y_done, c.at(1, 1))
                        ln_stats(2, c, y)
                    if j == 0 and st.mid:
                        c = st.mid
                        dve.wait_ge(ln_pool[1], c.at(2, 2))
                        if not (isinstance(c.number, int) and c.number < 2):
                            dve.wait_ge(x3_turned, c.number - 1)
                        for s in range(CHUNK):
                            nc.vector.tensor_scalar(x3[c.parity][:, s, :, :],
                                                    h2[c.parity][:, s:s + 1, :].to_broadcast([P, 2, C]),
                                                    mv[1][:, s, 0:1], rstd[1][:, s:s + 1],
                                                    ALU.subtract, ALU.mult).then_inc(x3_done, 1)
                    if j == 1 and st.old:
                        c = st.old
                        dve.wait_ge(ln_pool[2], c.at(2, 2))
                        wait(dve, yg_done, c.before(1))
                        for s in range(CHUNK):
                            nc.vector.tensor_scalar(yn[:, s, :], y[:, s, :], mv[2][:, s, 0:1], rstd[2][:, s:s + 1],
                                                    ALU.subtract, ALU.mult).then_inc(yn_done, 1)
                    if j == 1 and st.mid:
                        c = st.mid
                        dve.wait_ge(x3_high, c.at(1, 1))
                        low = x3_t[c.parity][C:2 * C, :]
                        nc.vector.tensor_tensor(low, bank_d[C:2 * C, :], low.bitcast(F32), ALU.subtract)\
                          .then_inc(x3_low, 1)
                    if j == 2 and st.old:
                        c = st.old
                        dve.wait_ge(yg_done, c.at(1, 1))
                        dve.wait_ge(h2b_done, c.at(1, 1))
                        wait(dve, stored, c.before(16))
                        nc.vector.tensor_tensor(res[:], yg[:], h2b[:], ALU.add).then_inc(res_done, 1)
                    if j == 2 and st.mid:
                        c = st.mid
                        n = 1
                        dve.wait_ge(logits_done, c.at(1, 1))
                        nc.vector.tensor_tensor(logits[:], bank_d[:, 0:CHUNK * E].rearrange("p (s e) -> p s e", s=CHUNK),
                                                gate_bias[:].unsqueeze(1).to_broadcast([P, CHUNK, E]), ALU.add)\
                          .then_inc(gate_step, 1)
                        dve.wait_ge(gate_step, c.at(N_GATE, 1))
                        fixed(dve)
                        for s in range(CHUNK):
                            nc.vector.max(top[:, s, :], logits[:, s, :]).then_inc(gate_step, 1)
                        dve.wait_ge(gate_step, c.at(N_GATE, 1 + CHUNK))
                        fixed(dve)
                        for s in range(CHUNK):
                            nc.vector.max_index(top_at[:, s, :], top[:, s, :], logits[:, s, :]).then_inc(gate_step, 1)
                        nc.vector.tensor_tensor(gap[:], top[:, :, 1], top[:, :, 0], ALU.subtract).then_inc(gate_step, 1)
                        dve.wait_ge(gate_step, c.at(N_GATE, 2 + 2 * CHUNK))
                        nc.vector.tensor_tensor(chosen[:],
                                                iota[:].unsqueeze(1).unsqueeze(1).to_broadcast([P, CHUNK, 2, E]),
                                                top_at[:, :, 0:2].unsqueeze(3).to_broadcast([P, CHUNK, 2, E]),
                                                ALU.is_equal).then_inc(gate_step, 1)
                        dve.wait_ge(gap_done, c.at(1, 1))
                        nc.vector.tensor_scalar(gap_sum[:], gap_exp[:], 1.0, None, ALU.add).then_inc(gate_step, 1)
                        dve.wait_ge(gate_step, c.at(N_GATE, 4 + 2 * CHUNK))
                        nc.vector.reciprocal(top_w[:, :, 0], gap_sum[:]).then_inc(gate_step, 1)
                        dve.wait_ge(gate_step, c.at(N_GATE, 5 + 2 * CHUNK))
                        nc.vector.tensor_tensor(top_w[:, :, 1], gap_exp[:], top_w[:, :, 0], ALU.mult)\
                          .then_inc(gate_step, 1)
                        dve.wait_ge(gate_step, c.at(N_GATE, 6 + 2 * CHUNK))
                        nc.vector.tensor_tensor(weighed[:], chosen[:],
                                                top_w[:].unsqueeze(3).to_broadcast([P, CHUNK, 2, E]), ALU.mult)\
                          .then_inc(gate_step, 1)
                        dve.wait_ge(gate_step, c.at(N_GATE, 7 + 2 * CHUNK))
                        wait(dve, gates_turned, c.before(1))
                        nc.vector.tensor_tensor(gates[:], weighed[:, :, 0, :], weighed[:, :, 1, :], ALU.add)\
                          .then_inc(x3_low, 1)
                    if j == 3 and st.new:
                        c = st.new
                        dve.wait_ge(pv_done, c.at(1, 1))
                        pv = bank_a[:, 0:CHUNK * (C + 1)].rearrange("p (s c) -> p s c", s=CHUNK)
                        nc.vector.reciprocal(rsum[:], pv[:, :, C]).then_inc(x1_step, 1)
                        dve.wait_ge(x1_step, c.at(N_X1, 1))
                        wait(dve, h1b_done, c.before(1))
                        nc.vector.tensor_tensor(h1[:], pv[:, :, 0:C], rsum[:].unsqueeze(2).to_broadcast([P, CHUNK, C]),
                                                ALU.mult).then_inc(x1_step, 1)
                        dve.wait_ge(x1_step, c.at(N_X1, 2))
                        ln_stats(0, c, h1)
                        dve.wait_ge(ln_pool[0], c.at(2, 2))
                        wait(dve, x1_turned, c.before(1))
                        for s in range(CHUNK):
                            ins = nc.vector.tensor_scalar(x1[:, s, 0:C], h1[:, s, :], mv[0][:, s, 0:1], rstd[0][:, s:s + 1],
                                                          ALU.subtract, ALU.mult)
                        ins.then_inc(x1_step, 1)
                    if j == 5 and st.new:
                        c = st.new
                        dve.wait_ge(squared, c.at(2, 2))
                        nc.vector.tensor_reduce(sq_sum[:], sq[:].rearrange("p s (a c) -> p (s a) c", a=2), AX.X, ALU.add)\
                          .then_inc(q_step, 1)
                        dve.wait_ge(q_step, c.at(N_Q, 1))
                        nc.vector.tensor_scalar(sq_sum[:], sq_sum[:], SUM_EPS, None, ALU.add).then_inc(q_step, 1)
                        dve.wait_ge(q_step, c.at(N_Q, 2))
                        nc.vector.reciprocal(sq_rec[:], sq_sum[:]).then_inc(q_step, 1)
                        dve.wait_ge(q_step, c.at(N_Q, 3))
                        wait(dve, kv_done, c.before(1))
                        nc.vector.tensor_tensor(qkv2[:, :, 0:2 * C].rearrange("p s (a c) -> p s a c", a=2),
                                                sq[:].rearrange("p s (a c) -> p s a c", a=2),
                                                sq_rec[:].rearrange("p (s a) -> p s a", a=2).unsqueeze(3)
                                                .to_broadcast([P, CHUNK, 2, C]), ALU.mult).then_inc(q_step, 1)
                        dve.wait_ge(q4_done, c.at(1, 1))
                        nc.vector.tensor_reduce(q4_sum[:], q4[:], AX.X, ALU.add).then_inc(q_step, 1)
                        dve.wait_ge(q_pool, c.at(2, 2))
                        wait(dve, q_turned, c.before(1))
                        nc.vector.tensor_tensor(q2n[:].rearrange("p a h c -> p h a c"),
                                                qkv2[:, :, 0:C].rearrange("p (h a) c -> p h a c", h=2),
                                                q_rn[:].rearrange("p (h a) -> p h a", h=2).unsqueeze(3)
                                                .to_broadcast([P, 2, PAIRS, C]), ALU.mult).then_inc(q_step, 1)
                    if j == 6 and st.new:
                        c = st.new
                        dve.wait_ge(kv_done, c.at(1, 1))
                        both = bank_a[:, 0:PAIRS * 2 * C].rearrange("p (s n) -> p s n", s=PAIRS)
                        nc.vector.tensor_tensor(gram[:], both[:, :, 0:C],
                                                ident2[:].unsqueeze(1).to_broadcast([P, PAIRS, C]), ALU.mult)\
                          .then_inc(k_step, 1)
                        dve.wait_ge(k_step, c.at(N_K, 1))
                        nc.vector.tensor_reduce(k_sum[:], gram[:], AX.X, ALU.add).then_inc(k_step, 1)
                        dve.wait_ge(k_pool, c.at(2, 2))
                        wait(dve, t2_done, c.before(1))
                        nc.vector.scalar_tensor_tensor(kv[:], both[:, :, C:2 * C], KV_SCALE,
                                                       k_rn[:].unsqueeze(2).to_broadcast([P, PAIRS, C]),
                                                       ALU.mult, ALU.mult).then_inc(k_step, 1)

            steps(dve, CHUNKS, body)

        @block.tensor
        def _(pe):
            pe.wait_ge(const_set, 7)
            pe.wait_ge(setup_dve, 1)
            pe.transpose(bank_d[:, 0:SEQS], x_f[:], ident[0:SEQS, 0:SEQS]).then_inc(setup_pe, 1)
            pe.wait_ge(emb_in, 16)
            for t in range(VT):
                bank = bank_a if t < VT // 2 else bank_acc
                ins = pe.transpose(bank[0:C, t % (VT // 2) * P:(t % (VT // 2) + 1) * P], emb_s[:, t, :], ident[:])
                if t % (VT // 2) == VT // 2 - 1:
                    ins.then_inc(setup_pe, 1)
            pe.wait_ge(tokw_in, 6 * 16)
            pe.wait_ge(setup_dve, 4)
            for t in range(VT):
                pe.wait_ge(emb_t_set, 1 + t // (VT // 2))
                if t >= 2:
                    pe.wait_ge(table_ev, t - 1)
                pe.matmul((bank_b if t % 2 == 0 else bank_c)[:, 0:3 * C], emb_t[:, t * P:(t + 1) * P], tok_w[:],
                          start=True, stop=True).then_inc(table_mm, 1)
            pe.wait_ge(small_in, 16 * 12)
            pe.transpose(bank_z[0][0:C, 0:C + 1], qkv_w[:, 2 * C:3 * C], ident[0:C + 1, 0:C + 1])
            pe.transpose(bank_z[0][:, 128:128 + E], b1_s[:], ident[0:E, 0:E]).then_inc(setup_pe, 1)
            pe.wait_ge(setup_dve, 14)
            pe.matmul(bank_z[1][0:C + 1, 0:C], wv_t[:], wout[:], start=True, stop=True).then_inc(setup_pe, 1)
            for e in range(E):
                ins = pe.matmul(bank_z[2][0:E, 0:C], b1_diag[:, e, :], w2_s[:, e, :], start=(e == 0), stop=(e == E - 1))
            ins.then_inc(setup_pe, 1)
            pe.wait_ge(setup_dve, 16)
            pe.wait_ge(ones_set, 3)

            def half_of(s):
                return s // PAIRS, s % PAIRS

            order = [0, 2, 1, 3]

            def turn_qk(c):
                pe.wait_ge(gathered[c.parity], 64 * (c.half + 1))
                for s in range(CHUNK):
                    ins = pe.transpose(bank_a[:, s * P:(s + 1) * P], gath[c.parity][:, s, 0:2 * C], ident[:])
                ins.then_inc(qk_turned, 1)

            def scores(c):
                pe.wait_ge(qk_copied, c.at(4, 4))
                wait(pe, h2_done, c.before(2))
                for s in order:
                    half, pair = half_of(s)
                    rows = slice(half * C, (half + 1) * C)
                    ins = pe.matmul((bank_b, bank_c)[half][:, pair * P:(pair + 1) * P], qk_t[rows, 1, pair, :],
                                    qk_t[rows, 0, pair, :], start=True, stop=True)
                ins.then_inc(scored, 1)

            def p_v(c):
                pe.wait_ge(exp_done, c.at(2, 2))
                for s in range(CHUNK):
                    ins = pe.matmul(bank_a[:, s * (C + 1):(s + 1) * (C + 1)], probs[:, s, :],
                                    gath[c.parity][:, s, 2 * C:3 * C + 1], start=True, stop=True)
                ins.then_inc(pv_done, 1)

            def turn_x1(c):
                pe.wait_ge(x1_step, c.at(N_X1, 3))
                for s in range(CHUNK):
                    ins = pe.transpose(bank_a[0:C + 1, s * P:(s + 1) * P], x1[:, s, :], ident[:])
                ins.then_inc(x1_turned, 1)

            def q_k_v(c):
                pe.wait_ge(x1_copied, c.at(1, 1))
                for s in range(CHUNK):
                    half, pair = half_of(s)
                    ins = pe.matmul((bank_b, bank_c)[half][:, pair * 3 * C:(pair + 1) * 3 * C],
                                    x1_t[:, s * P:(s + 1) * P], qkv_w[:], start=(pair == 0), stop=(pair == PAIRS - 1),
                                    skip_group_check=True)
                ins.then_inc(qkv_done, 1)

            def k_v(c):
                pe.wait_ge(q_step, c.at(N_Q, 4))
                pe.wait_ge(v_copied, c.at(2, 2))
                for s in order:
                    half, pair = half_of(s)
                    ins = pe.matmul(bank_a[half * C:(half + 1) * C, pair * 2 * C:(pair + 1) * 2 * C],
                                    qkv2[:, s, C:2 * C], qkv2[:, s, C:3 * C], start=True, stop=True)
                ins.then_inc(kv_done, 1)

            def turn_q(c):
                pe.wait_ge(q_step, c.at(N_Q, 6))
                wait(pe, gates_copied, c.before(1))
                for pair in range(PAIRS):
                    ins = pe.transpose(bank_d[:, pair * P:(pair + 1) * P], 
                                       q2n[:, pair, :, :].rearrange("p h c -> p (h c)"), ident[:])
                ins.then_inc(q_turned, 1)

            def add_t2(c):
                pe.wait_ge(k_step, c.at(N_K, 3))
                pe.wait_ge(q_copied, c.at(1, 1))
                for s in order:
                    half, pair = half_of(s)
                    rows = slice(half * C, (half + 1) * C)
                    at = pair * 3 * C + 2 * C
                    ins = pe.matmul((bank_b, bank_c)[half][:, at:at + C], q2n_t[rows, pair, :], kv[rows, pair, :],
                                    start=False, stop=True, skip_group_check=True)
                ins.then_inc(t2_done, 1)

            def turn_x3(c):
                pe.wait_ge(x3_done, c.at(CHUNK, CHUNK))
                for s in range(CHUNK):
                    ins = pe.transpose(bank_d[:, s * P:(s + 1) * P], x3[c.parity][:, s, :, :].rearrange("p a c -> p (a c)"), ident[:])
                ins.then_inc(x3_turned, 1)

            def gate_logits(c):
                pe.wait_ge(x3_low, c.at(2, 1))
                for s in range(CHUNK):
                    for i, w in enumerate((gate_hi, gate_lo)):
                        ins = pe.matmul(bank_d[:, s * E:(s + 1) * E], x3_t[c.parity][:, s * P:(s + 1) * P], w[:],
                                        start=(i == 0), stop=(i == 1))
                ins.then_inc(logits_done, 1)

            def turn_gates(c):
                pe.wait_ge(x3_low, c.at(2, 2))
                for s in range(CHUNK):
                    ins = pe.transpose(bank_d[0:E, s * P:(s + 1) * P], gates[:, s, :], ident[:])
                ins.then_inc(gates_turned, 1)

            def hidden_mm(c, e):
                if e >= Z_BANKS:
                    pe.wait_ge(hidden_ready, c.at(E, e - Z_BANKS + 1))
                elif c.before(E) is not None:
                    last = max(n for n in range(E) if n % Z_BANKS == e % Z_BANKS)
                    pe.wait_ge(hidden_ready, c.before(E, last + 1))
                for i, w in enumerate((w1_hi, w1_lo)):
                    ins = pe.matmul(bank_z[e % Z_BANKS][:], w[:, e * F:(e + 1) * F], x3_t[c.parity][:],
                                    start=(i == 0), stop=(i == 1))
                ins.then_inc(z_ready, 1)

            def out_mm(c, j):
                if j == 0:
                    wait(pe, acc_copied, c.before(1))
                    pe.wait_ge(gates_copied, c.at(1, 1))
                    pe.matmul(bank_acc[0:C, :], gate_const[:], gates_t[c.parity][:], start=True, stop=False,
                              skip_group_check=True)
                for e in (2 * j, 2 * j + 1):
                    half = e % 2
                    pe.wait_ge(hidden_ready, c.at(E, e + 1))
                    pe.matmul(bank_acc[half * C:(half + 1) * C, :], w2_s[:, e, :], hidden[e % RING][:],
                              start=(e == 1), stop=(e >= E - 2), skip_group_check=True).then_inc(hidden_used, 1)

            def sum_halves(c):
                pe.wait_ge(acc_copied, c.at(1, 1))
                for s in range(CHUNK):
                    ins = pe.matmul(bank_a[:, s * C:(s + 1) * C], moe_t[:, s * P:(s + 1) * P], ident2[:],
                                    start=True, stop=True)
                ins.then_inc(moe_done, 1)

            def body(st):
                for j in range(SLOTS):
                    if st.moe:
                        hidden_mm(st.moe, 2 * j)
                        hidden_mm(st.moe, 2 * j + 1)
                    if j == 0:
                        if st.mid:
                            add_t2(st.mid)
                        if st.old:
                            sum_halves(st.old)
                    if j == 1:
                        if st.mid:
                            turn_x3(st.mid)
                        if st.new:
                            wait(pe, y_done, None if st.old is None else st.old.at(1, 1))
                            turn_qk(st.new)
                    if j == 2:
                        if st.mid:
                            gate_logits(st.mid)
                        if st.new:
                            scores(st.new)
                    if j == 3:
                        if st.mid:
                            turn_gates(st.mid)
                        if st.new:
                            p_v(st.new)
                    if st.new:
                        if j == 4:
                            turn_x1(st.new)
                        if j == 5:
                            q_k_v(st.new)
                        if j == 6:
                            k_v(st.new)
                        if j == 7:
                            turn_q(st.new)
                    if st.moe and j > 0:
                        out_mm(st.moe, j - 1)
                if st.moe:
                    out_mm(st.moe, SLOTS - 1)

            steps(pe, CHUNKS, body)


_INS = ["x", "L0_tok_emb_table", "L0_tok_Wq", "L0_tok_bq", "L0_tok_Wk", "L0_tok_bk", "L0_tok_Wv", "L0_tok_bv",
        "L0_attn_W_qkv", "L0_attn_b_qkv", "L0_attn_W_out", "L0_attn_b_out", "L0_ffn_gate_w", "L0_ffn_gate_b",
        "L0_ffn_w1", "L0_ffn_b1", "L0_ffn_w2", "L0_ffn_b2", "L0_ffn_gamma", "L0_ffn_beta"]


def kernel(**inputs):
    import numpy as np
    import concourse.bacc as bacc
    from concourse import mybir as _mybir
    from concourse.bass_utils import run_bass_kernel_spmd as run

    nc = bacc.Bacc("TRN2", target_bir_lowering=False, num_devices=1)
    arrays, args = {}, []
    for name in _INS:
        a = np.ascontiguousarray(inputs[name])
        arrays[f"in_{name}"] = a
        args.append(nc.dram_tensor(f"in_{name}", a.shape, _mybir.dt.from_np(a.dtype), kind="ExternalInput").ap())
    shape = (*inputs["x"].shape, inputs["L0_tok_emb_table"].shape[1])
    args.append(nc.dram_tensor("out_0", shape, _mybir.dt.float32, kind="ExternalOutput").ap())
    build(nc, *args)
    r = run(nc, [arrays], core_ids=[0])
    return r.results[0]["out_0"]
```

```python
from contextlib import ExitStack

import concourse.bass as bass
from concourse import mybir

F32 = mybir.dt.float32
F32R = mybir.dt.float32r
I32 = mybir.dt.int32
U32 = mybir.dt.uint32
ACT = mybir.ActivationFunctionType
ALU = mybir.AluOpType
AX = mybir.AxisListType

P = 128
CHUNK = 4
PAIRS = CHUNK // 2
SLOTS = 8
Z_BANKS = 3
RING = 4
PARTS = 4
LN_EPS = 1e-5
SUM_EPS = 1e-7
NORM_EPS = 1e-12


class Chunk:

    def __init__(self, number, half, parity):
        self.number, self.half, self.parity = number, half, parity

    def at(self, per_chunk, n):
        return self.number * per_chunk + n

    def before(self, per_chunk, n=None):
        if isinstance(self.number, int) and self.number == 0:
            return None
        return (self.number - 1) * per_chunk + (per_chunk if n is None else n)


class Step:

    def __init__(self, k, chunks, m=None):
        def chunk(off):
            n = k + off
            if m is not None:
                return Chunk(2 * m + n, m + n // 2, n % 2)
            return Chunk(n, n // 2, n % 2) if 0 <= n < chunks else None

        self.old, self.moe, self.gate, self.linear, self.attend, self.fetch = (chunk(o) for o in range(-1, 5))
        self.at = {"old": self.old, "moe": self.moe, "gate": self.gate, "linear": self.linear,
                   "attend": self.attend, "fetch": self.fetch}


def steps(engine, chunks, body):
    first, last = 2, (chunks - 4) // 2 * 2
    for k in range(-4, first):
        body(Step(k, chunks))
    with engine.Fori(first // 2, last // 2) as m:
        body(Step(0, chunks, m))
        body(Step(1, chunks, m))
    for k in range(last, chunks + 1):
        body(Step(k, chunks))


def wait(engine, semaphore, value):
    if value is not None:
        engine.wait_ge(semaphore, value)


def build(nc, x, emb, Wq, bq, Wk, bk, Wv, bv, W_qkv, b_qkv, W_out, b_out,
          gate_w, gate_b, w1, b1, w2, b2, gamma, beta, out):
    SEQS, T = x.shape
    VOCAB, C = emb.shape
    E, _, F = w1.shape
    CHUNKS = SEQS // CHUNK
    TOK = CHUNK * T
    VT = VOCAB // P
    GW = 200
    assert T == P and F == P and C == 64 and E == 2 * SLOTS and CHUNKS % 2 == 0
    SCORE_SCALE = float(C) ** -0.5
    KV_SCALE = float(T) ** -0.5
    SMALL = 16 * 12
    N_CONST = 13

    gates_dram = [nc.dram_tensor(f"gates{i}", (E, TOK), F32, kind="Internal").ap() for i in range(2)]
    table = nc.dram_tensor("qkv_table", (VOCAB, 3 * C), F32, kind="Internal").ap()

    with ExitStack() as ctx:
        def sb(name, shape, dt=F32):
            return ctx.enter_context(nc.sbuf_tensor(name, shape, dt))

        def ps(name):
            return ctx.enter_context(nc.psum_tensor(name, [P, 512], F32))

        def sem(name):
            return ctx.enter_context(nc.semaphore(name))

        bank_a, bank_b, bank_c, bank_d, bank_acc = (ps(n) for n in ("bank_a", "bank_b", "bank_c", "bank_d", "bank_acc"))
        bank_z = [ps(f"bank_z{i}") for i in range(Z_BANKS)]

        ident = sb("ident", [P, P])
        ident2 = sb("ident2", [P, C])
        iota = sb("iota", [P, E])
        iota_i = sb("iota_i", [P, E], I32)
        ident2_r = sb("ident2_r", [P, C], F32R)
        ones = sb("ones", [P, 1])
        minus_half = sb("minus_half", [P, CHUNK])
        tok_w = sb("tok_w", [C + 1, 3 * C])
        qkv_w = sb("qkv_w", [C + 1, 3 * C])
        wout = sb("wout", [C, C])
        wv_t = sb("wv_t", [C, C + 1])
        qk_mean = sb("qk_mean", [C + 1, 2])
        gate_s = sb("gate_s", [P, E])
        gate_bias = sb("gate_bias", [P, E])
        w1_raw = sb("w1_raw", [P, E * F])
        w1_hi = sb("w1_hi", [P, E * F], F32R)
        w1_lo = sb("w1_lo", [P, E * F], F32R)
        w2_s = sb("w2_s", [P, E, C])
        b1_s = sb("b1_s", [E, F])
        b1_neg = sb("b1_neg", [P, E])
        b1_diag = sb("b1_diag", [P, E, E])
        b2_s = sb("b2_s", [E, C])
        gate_const = sb("gate_const", [E, C])
        out_bias = sb("out_bias", [P, C])
        gamma_s = sb("gamma_s", [P, C])
        beta_s = sb("beta_s", [P, C])
        emb_s = sb("emb_s", [P, VT, C])
        emb_t = sb("emb_t", [C + 1, VOCAB])
        table_s = sb("table_s", [P, VT, 3 * C])
        x_s = sb("x_s", [SEQS, T], I32)
        x_f = sb("x_f", [SEQS, T])
        tok_id = sb("tok_id", [P, SEQS], I32)
        rows_now = [sb(f"rows_now{i}", [P, CHUNK], I32) for i in range(2)]
        gath = [sb(f"gath{i}", [P, CHUNK, GW]) for i in range(2)]
        qk_t = sb("qk_t", [C, 2, TOK])
        probs = sb("probs", [P, CHUNK, P])
        rsum = sb("rsum", [P, CHUNK])
        h1 = sb("h1", [P, CHUNK, C])
        h1b = [sb(f"h1b{i}", [P, CHUNK, C]) for i in range(2)]
        x1 = sb("x1", [P, CHUNK, C + 1])
        x1_t = sb("x1_t", [C + 1, TOK])
        sq = sb("sq", [P, CHUNK, 2 * C])
        v = sb("v", [P, CHUNK, C])
        sq_sum = sb("sq_sum", [P, 2 * CHUNK])
        sq_rec = sb("sq_rec", [P, 2 * CHUNK])
        k2 = sb("k2", [P, CHUNK, C])
        k4 = sb("k4", [P, CHUNK, C])
        q4 = sb("q4", [P, CHUNK, C])
        q4_sum = sb("q4_sum", [P, CHUNK])
        q4_max = sb("q4_max", [P, CHUNK])
        q_rn = sb("q_rn", [P, CHUNK])
        q_scale = sb("q_scale", [P, CHUNK])
        q2n = sb("q2n", [P, PAIRS, 2, C])
        q2n_t = sb("q2n_t", [P, PAIRS, P])
        k_max = sb("k_max", [P, PAIRS])
        k_rn = sb("k_rn", [P, PAIRS])
        kv = sb("kv", [P, PAIRS, C])
        h2 = [sb(f"h2{i}", [P, CHUNK, C]) for i in range(2)]
        h2b = [sb(f"h2b{i}", [P, CHUNK, C]) for i in range(2)]
        x3 = sb("x3", [P, CHUNK, C])
        x3_parts = sb("x3_parts", [P, CHUNK, 2, C])
        x3_t = [sb(f"x3_t{i}", [P, TOK], F32R) for i in range(2)]
        logits = sb("logits", [P, CHUNK, E])
        top = sb("top", [P, CHUNK, 8])
        top_at = sb("top_at", [P, CHUNK, 8], U32)
        gap = sb("gap", [P, CHUNK])
        gap_exp = sb("gap_exp", [P, CHUNK])
        gap_sum = sb("gap_sum", [P, CHUNK])
        top_w = sb("top_w", [P, CHUNK, 2])
        chosen = sb("chosen", [P, CHUNK, 2, E])
        weighed = sb("weighed", [P, CHUNK, 2, E])
        gates = sb("gates", [P, CHUNK, E])
        gates_t = [sb(f"gates_t{i}", [E, TOK]) for i in range(2)]
        spread = [sb(f"spread{i}", [P, E * TOK]) for i in range(2)]
        hidden = [sb(f"hidden{i}", [P, TOK]) for i in range(RING)]
        acc = sb("acc", [P, TOK])
        y = sb("y", [P, CHUNK, C])
        yn = sb("yn", [P, CHUNK, C])
        yg = sb("yg", [P, CHUNK, C])
        res = sb("res", [P, CHUNK, C])
        stats = [sb(f"stats{i}", [P, CHUNK, 6]) for i in range(3)]
        mv = [sb(f"mv{i}", [P, CHUNK, 2]) for i in range(3)]
        var = [sb(f"var{i}", [P, CHUNK]) for i in range(3)]
        neg_mean = [sb(f"neg_mean{i}", [P, CHUNK]) for i in range(3)]
        rstd = [sb(f"rstd{i}", [P, CHUNK]) for i in range(3)]
        shift = [sb(f"shift{i}", [P, CHUNK]) for i in range(3)]

        x_in = sem("x_in")
        emb_in = sem("emb_in")
        tokw_in = sem("tokw_in")
        small_in = sem("small_in")
        w1_in = sem("w1_in")
        const_set = sem("const_set")
        x_f_set = sem("x_f_set")
        x_turned = sem("x_turned")
        tok_set = sem("tok_set")
        emb_turned = sem("emb_turned")
        emb_t_set = sem("emb_t_set")
        table_mm = sem("table_mm")
        table_ev = sem("table_ev")
        table_out = sem("table_out")
        centred = sem("centred")
        split = sem("split")
        b_turned = sem("b_turned")
        b1_set = sem("b1_set")
        fused = sem("fused")
        fused_set = sem("fused_set")
        qk_turned = sem("qk_turned")
        scored = sem("scored")
        pv_done = sem("pv_done")
        x1_turned = sem("x1_turned")
        qkv_done = sem("qkv_done")
        kv_done = sem("kv_done")
        q_turned = sem("q_turned")
        t2_done = sem("t2_done")
        x3_turned = sem("x3_turned")
        logits_done = sem("logits_done")
        gates_turned = sem("gates_turned")
        z_ready = sem("z_ready")
        hidden_used = sem("hidden_used")
        acc_turned = sem("acc_turned")
        qk_copied = sem("qk_copied")
        exp_done = sem("exp_done")
        x1_done = sem("x1_done")
        x1_copied = sem("x1_copied")
        squared = sem("squared")
        v_copied = sem("v_copied")
        q4_done = sem("q4_done")
        k4_done = sem("k4_done")
        q2n_done = sem("q2n_done")
        q_copied = sem("q_copied")
        x3_done = sem("x3_done")
        x3_high = sem("x3_high")
        x3_copied = sem("x3_copied")
        gap_done = sem("gap_done")
        gates_copied = sem("gates_copied")
        acc_copied = sem("acc_copied")
        yn_done = sem("yn_done")
        ln_stat = [sem(f"ln_stat{i}") for i in range(3)]
        h1_step = sem("h1_step")
        q_step = sem("q_step")
        k_step = sem("k_step")
        h2_done = sem("h2_done")
        y_done = sem("y_done")
        gate_step = sem("gate_step")
        hidden_ready = sem("hidden_ready")
        rows_set = sem("rows_set")
        ln_pool = [sem(f"ln_pool{i}") for i in range(3)]
        h1b_done = sem("h1b_done")
        q_pool = sem("q_pool")
        k_pool = sem("k_pool")
        x3_low = sem("x3_low")
        pool_gate = sem("pool_gate")
        h2b_done = sem("h2b_done")
        yg_done = sem("yg_done")
        res_done = sem("res_done")
        gathered = [sem(f"gathered{i}") for i in range(2)]
        gates_out = [sem(f"gates_out{i}") for i in range(2)]
        spread_in = [[sem(f"spread_in{i}_{n}") for n in range(PARTS)] for i in range(2)]
        stored = sem("stored")

        N_Q, N_K, N_LN, N_GATE = 4, 2, 4, 6 + 2 * CHUNK

        def fixed(engine):
            engine.nop(nofuse=True)

        block = ctx.enter_context(nc.Block())

        @block.sync
        def _(sp):
            sp.dma_start(x_s[:], x).then_inc(x_in, 16)
            sp.dma_start(emb_s[:], emb.rearrange("(t p) c -> p t c", p=P)).then_inc(emb_in, 16)
            for i, (w, b) in enumerate(((Wq, bq), (Wk, bk), (Wv, bv))):
                sp.dma_start(tok_w[0:C, i * C:(i + 1) * C], w).then_inc(tokw_in, 16)
                sp.dma_start(tok_w[C:C + 1, i * C:(i + 1) * C], b.rearrange("(a c) -> a c", a=1)).then_inc(tokw_in, 16)
            sp.dma_start(qkv_w[0:C, :], W_qkv).then_inc(small_in, 16)
            sp.dma_start(qkv_w[C:C + 1, :], b_qkv.rearrange("(a c) -> a c", a=1)).then_inc(small_in, 16)
            sp.dma_start(wout[:], W_out).then_inc(small_in, 16)
            sp.dma_start(out_bias[:], b_out.partition_broadcast(P)).then_inc(small_in, 16)
            sp.dma_start(b1_s[:], b1).then_inc(small_in, 16)
            sp.dma_start(b2_s[:], b2).then_inc(small_in, 16)
            sp.dma_start(w2_s[:], w2.rearrange("e f c -> f e c")).then_inc(small_in, 16)
            for half in range(2):
                sp.dma_start(gate_s[half * C:(half + 1) * C, :], gate_w).then_inc(small_in, 16)
                sp.dma_start(w1_raw[half * C:(half + 1) * C, :].rearrange("c (e f) -> c e f", e=E),
                             w1.rearrange("e c f -> c e f")).then_inc(w1_in, 16)
            sp.dma_start(gate_bias[:], gate_b.partition_broadcast(P)).then_inc(small_in, 16)
            sp.dma_start(gamma_s[:], gamma.partition_broadcast(P)).then_inc(small_in, 16)
            sp.dma_start(beta_s[:], beta.partition_broadcast(P)).then_inc(small_in, 16)
            sp.wait_ge(table_ev, VT)
            sp.dma_start(table.rearrange("(t p) c -> p t c", p=P), table_s[:]).then_inc(table_out, 16)

            def body(st):
                if st.gate:
                    c = st.gate
                    sp.wait_ge(gates_copied, c.at(1, 1))
                    fixed(sp)
                    if not (isinstance(c.number, int) and c.number < 2):
                        sp.wait_ge(hidden_ready, (c.number - 1) * E)
                    sp.dma_start(gates_dram[c.parity], gates_t[c.parity][:]).then_inc(gates_out[c.parity], 16)
                    sp.wait_ge(gates_out[c.parity], 16 * (c.half + 1))
                    n = E // PARTS
                    for i in range(PARTS):
                        rows = gates_dram[c.parity][i * n:(i + 1) * n, :].rearrange("e t -> (e t)")
                        sp.dma_start(spread[c.parity][:, i * n * TOK:(i + 1) * n * TOK], rows.partition_broadcast(P))\
                          .then_inc(spread_in[c.parity][i], 16)
                if st.old:
                    c = st.old
                    sp.wait_ge(res_done, c.at(1, 1))
                    fixed(sp)
                    rows = out[bass.ds(c.number * CHUNK, CHUNK), :, :].rearrange("s t c -> t s c")
                    sp.dma_start(rows, res[:]).then_inc(stored, 16)

            steps(sp, CHUNKS, body)
            sp.wait_ge(stored, 16 * CHUNKS)

        @block.gpsimd
        def _(pool):
            nc.gpsimd.memset(ident[:], 0.0).then_inc(const_set, 1)
            nc.gpsimd.memset(ident2[:], 0.0).then_inc(const_set, 1)
            nc.gpsimd.memset(minus_half[:], -0.5).then_inc(const_set, 1)
            nc.gpsimd.iota(iota_i[:], pattern=[[1, E]], base=0, channel_multiplier=0).then_inc(const_set, 1)
            pool.wait_ge(const_set, 4)
            nc.gpsimd.affine_select(out=ident[:], in_=ident[:], compare_op=ALU.not_equal, fill=1.0, base=0,
                                    pattern=[[-1, P]], channel_multiplier=1).then_inc(const_set, 1)
            nc.gpsimd.affine_select(out=ident2[:], in_=ident2[:], compare_op=ALU.not_equal, fill=1.0, base=0,
                                    pattern=[[-1, C]], channel_multiplier=1).then_inc(const_set, 1)
            pool.wait_ge(const_set, 6)
            nc.gpsimd.affine_select(out=ident2[:], in_=ident2[:], compare_op=ALU.not_equal, fill=1.0, base=-C,
                                    pattern=[[-1, C]], channel_multiplier=1).then_inc(const_set, 1)
            nc.gpsimd.tensor_copy(iota[:], iota_i[:]).then_inc(const_set, 1)
            nc.gpsimd.memset(ones[:], 1.0).then_inc(const_set, 1)
            nc.gpsimd.memset(b1_diag[:], 0.0).then_inc(const_set, 1)
            nc.gpsimd.memset(x1[:, :, C:C + 1], 1.0).then_inc(const_set, 1)
            nc.gpsimd.memset(gath[0][:, :, 3 * C:3 * C + 1], 1.0).then_inc(const_set, 1)
            nc.gpsimd.memset(gath[1][:, :, 3 * C:3 * C + 1], 1.0).then_inc(const_set, 1)
            pool.wait_ge(small_in, SMALL)
            pool.wait_ge(table_out, 16)
            pool.wait_ge(tok_set, 1)

            def gather(c, first, last):
                if first == 0:
                    if not (isinstance(c.number, int) and c.number < 2):
                        pool.wait_ge(pv_done, c.number - 1)
                        pool.wait_ge(gathered[c.parity], 16 * CHUNK * c.half)
                    nc.gpsimd.tensor_copy(rows_now[c.parity][:], tok_id[:, bass.ds(c.number * CHUNK, CHUNK)])\
                      .then_inc(rows_set, 1)
                    pool.wait_ge(rows_set, c.at(1, 1))
                    fixed(pool)
                for s in range(first, last):
                    nc.gpsimd.indirect_dma_start(
                        gath[c.parity][:, s, 0:3 * C], None, table,
                        bass.IndirectOffsetOnAxis(ap=rows_now[c.parity][:, s:s + 1], axis=0),
                    ).then_inc(gathered[c.parity], 16)

            def ln_factors(i, c):
                pool.wait_ge(ln_stat[i], c.at(2 * CHUNK, 2 * CHUNK))
                fixed(pool)
                nc.gpsimd.tensor_scalar(var[i][:], mv[i][:, :, 1], LN_EPS, None, ALU.add).then_inc(ln_pool[i], 1)
                nc.gpsimd.tensor_scalar(neg_mean[i][:], mv[i][:, :, 0], -1.0, None, ALU.mult).then_inc(ln_pool[i], 1)
                pool.wait_ge(ln_pool[i], c.at(N_LN, 1))
                nc.gpsimd.tensor_tensor(rstd[i][:], var[i][:], minus_half[:], ALU.pow).then_inc(ln_pool[i], 1)
                pool.wait_ge(ln_pool[i], c.at(N_LN, 3))
                nc.gpsimd.tensor_tensor(shift[i][:], neg_mean[i][:], rstd[i][:], ALU.mult).then_inc(ln_pool[i], 1)

            def low_parts(c):
                pool.wait_ge(x3_high, c.at(1, 1))
                wait(pool, x3_turned, c.before(1))
                nc.gpsimd.tensor_tensor(x3_parts[:, :, 1, :], x3[:], x3_parts[:, :, 0, :], ALU.subtract)\
                  .then_inc(x3_low, 1)

            def q_factors(c):
                pool.wait_ge(q4_done, c.at(CHUNK, CHUNK))
                fixed(pool)
                nc.gpsimd.tensor_scalar(q4_max[:], q4_sum[:], NORM_EPS ** 2, None, ALU.max).then_inc(q_pool, 1)
                pool.wait_ge(q_pool, c.at(3, 1))
                nc.gpsimd.tensor_tensor(q_rn[:], q4_max[:], minus_half[:], ALU.pow).then_inc(q_pool, 1)
                pool.wait_ge(q_pool, c.at(3, 2))
                wait(pool, q2n_done, c.before(CHUNK))
                nc.gpsimd.tensor_tensor(q_scale[:], q_rn[:], sq_rec[:, 0:CHUNK], ALU.mult).then_inc(q_pool, 1)

            def k_factors(c):
                pool.wait_ge(k_step, c.at(N_K, 1))
                nc.gpsimd.tensor_tensor(k_rn[:], k_max[:], minus_half[:, 0:PAIRS], ALU.pow).then_inc(k_pool, 1)

            def add_out_bias(c):
                pool.wait_ge(h1_step, c.at(2, 2))
                if not (isinstance(c.number, int) and c.number < 2):
                    pool.wait_ge(h2_done, 2 * (c.number - 1))
                nc.gpsimd.tensor_tensor(h1b[c.parity][:], h1[:], out_bias[:].unsqueeze(1).to_broadcast([P, CHUNK, C]),
                                        ALU.add).then_inc(h1b_done, 1)

            def add_beta(c):
                pool.wait_ge(h2_done, c.at(2, 2))
                if not (isinstance(c.number, int) and c.number < 2):
                    pool.wait_ge(res_done, c.number - 1)
                nc.gpsimd.tensor_tensor(h2b[c.parity][:], h2[c.parity][:],
                                        beta_s[:].unsqueeze(1).to_broadcast([P, CHUNK, C]),
                                        ALU.add).then_inc(h2b_done, 1)

            def make_gates(c):
                pool.wait_ge(gate_step, c.at(N_GATE, N_GATE))
                nc.gpsimd.tensor_tensor(weighed[:], chosen[:], top_w[:].unsqueeze(3).to_broadcast([P, CHUNK, 2, E]),
                                        ALU.mult).then_inc(pool_gate, 1)
                pool.wait_ge(pool_gate, c.at(2, 1))
                wait(pool, gates_turned, c.before(1))
                nc.gpsimd.tensor_tensor(gates[:], weighed[:, :, 0, :], weighed[:, :, 1, :], ALU.add)\
                  .then_inc(pool_gate, 1)

            def result(c):
                pool.wait_ge(yn_done, c.at(CHUNK, CHUNK))
                nc.gpsimd.tensor_tensor(yg[:], yn[:], gamma_s[:].unsqueeze(1).to_broadcast([P, CHUNK, C]),
                                        ALU.mult).then_inc(yg_done, 1)
                pool.wait_ge(yg_done, c.at(1, 1))
                wait(pool, stored, c.before(16))
                nc.gpsimd.tensor_tensor(res[:], yg[:], h2b[c.parity][:], ALU.add).then_inc(res_done, 1)

            def body(st):
                if st.gate:
                    low_parts(st.gate)
                if st.fetch:
                    gather(st.fetch, 0, 3)
                if st.linear:
                    q_factors(st.linear)
                if st.moe:
                    add_beta(st.moe)
                if st.linear:
                    k_factors(st.linear)
                if st.attend:
                    add_out_bias(st.attend)
                if st.fetch:
                    gather(st.fetch, 3, 4)
                if st.gate:
                    make_gates(st.gate)
                if st.attend:
                    ln_factors(0, st.attend)
                if st.old:
                    ln_factors(2, st.old)
                if st.linear:
                    ln_factors(1, st.linear)
                if st.old:
                    result(st.old)

            steps(pool, CHUNKS, body)

        @block.scalar
        def _(act):
            for t in range(VT):
                act.wait_ge(table_mm, t + 1)
                nc.scalar.copy(table_s[:, t, :], (bank_b if t % 2 == 0 else bank_c)[:, 0:3 * C]).then_inc(table_ev, 1)

            def normalise(i, c, dst, src, done):
                act.wait_ge(ln_pool[i], c.at(N_LN, N_LN))
                for s in range(CHUNK):
                    nc.scalar.activation(dst[:, s, :], src[:, s, :], ACT.Identity, bias=shift[i][:, s:s + 1],
                                         scale=rstd[i][:, s:s + 1]).then_inc(done, 1)

            def copy_acc(c):
                act.wait_ge(hidden_used, c.at(E, E))
                wait(act, acc_turned, c.before(1))
                nc.scalar.copy(acc[:], bank_acc[:]).then_inc(acc_copied, 1)

            def copy_qk(c):
                act.wait_ge(qk_turned, c.at(1, 1))
                wait(act, scored, c.before(1))
                for i in range(2):
                    nc.scalar.copy(qk_t[:, i, :], bank_a[i * C:(i + 1) * C, :]).then_inc(qk_copied, 1)

            def exp_scores(c):
                act.wait_ge(scored, c.at(1, 1))
                wait(act, pv_done, c.before(1))
                nc.scalar.activation(probs[:].rearrange("p s t -> p (s t)"), bank_a[:], ACT.Exp, scale=SCORE_SCALE)\
                  .then_inc(exp_done, 1)

            def norm_h1(c):
                wait(act, x1_turned, c.before(1))
                normalise(0, c, x1[:, :, 0:C], h1, x1_done)

            def copy_x1(c):
                act.wait_ge(x1_turned, c.at(1, 1))
                wait(act, qkv_done, c.before(1))
                nc.scalar.copy(x1_t[:], bank_a[0:C + 1, :]).then_inc(x1_copied, 1)

            def square_qk(c):
                act.wait_ge(qkv_done, c.at(1, 1))
                wait(act, q_step, c.before(N_Q, N_Q))
                wait(act, kv_done, c.before(1))
                for half, bank in ((0, bank_b), (1, bank_c)):
                    both = bank[:, 0:2 * 3 * C].rearrange("p (s n) -> p s n", s=2)
                    nc.scalar.activation(sq[:, 2 * half:2 * half + 2, :], both[:, :, 0:2 * C], ACT.Square)\
                      .then_inc(squared, 1)
                    nc.scalar.copy(v[:, 2 * half:2 * half + 2, :], both[:, :, 2 * C:3 * C]).then_inc(v_copied, 1)

            def fourth_q(c):
                act.wait_ge(q_step, c.at(N_Q, 3))
                wait(act, q_pool, c.before(3))
                for s in range(CHUNK):
                    nc.scalar.activation(q4[:, s, :], sq[:, s, 0:C], ACT.Square, scale=sq_rec[:, s:s + 1],
                                         accum_out=q4_sum[:, s:s + 1]).then_inc(q4_done, 1)

            def fourth_k(c):
                act.wait_ge(q_step, c.at(N_Q, 4))
                wait(act, kv_done, c.before(1))
                nc.scalar.activation(k4[:], k2[:], ACT.Square).then_inc(k4_done, 1)

            def norm_q(c):
                act.wait_ge(q_pool, c.at(3, 3))
                wait(act, q_turned, c.before(1))
                for s in range(CHUNK):
                    half, pair = s // PAIRS, s % PAIRS
                    nc.scalar.activation(q2n[:, pair, half, :], sq[:, s, 0:C], ACT.Identity, scale=q_scale[:, s:s + 1])\
                      .then_inc(q2n_done, 1)

            def copy_q(c):
                act.wait_ge(q_turned, c.at(1, 1))
                wait(act, t2_done, c.before(1))
                nc.scalar.copy(q2n_t[:].rearrange("p a t -> p (a t)"), bank_d[:, 0:2 * P]).then_inc(q_copied, 1)

            def norm_h2(c):
                wait(act, x3_low, c.before(1))
                normalise(1, c, x3, h2[c.parity], x3_done)
                act.wait_ge(x3_done, c.at(CHUNK, CHUNK))
                wait(act, x3_turned, c.before(1))
                nc.scalar.copy(x3_parts[:, :, 0, :].bitcast(F32R), x3[:]).then_inc(x3_high, 1)

            def copy_x3(c):
                act.wait_ge(x3_turned, c.at(1, 1))
                if not (isinstance(c.number, int) and c.number < 2):
                    act.wait_ge(hidden_used, (c.number - 1) * E)
                nc.scalar.copy(x3_t[c.parity][:], bank_d[:]).then_inc(x3_copied, 1)

            def exp_gap(c):
                act.wait_ge(gate_step, c.at(N_GATE, 2 + 2 * CHUNK))
                nc.scalar.activation(gap_exp[:], gap[:], ACT.Exp).then_inc(gap_done, 1)

            def copy_gates(c):
                act.wait_ge(gates_turned, c.at(1, 1))
                if not (isinstance(c.number, int) and c.number < 2):
                    act.wait_ge(gates_out[c.parity], 16 * c.half)
                    act.wait_ge(hidden_used, (c.number - 1) * E)
                nc.scalar.copy(gates_t[c.parity][:], bank_a[0:E, :]).then_inc(gates_copied, 1)

            def norm_y(c):
                wait(act, yg_done, c.before(1))
                normalise(2, c, yn, y, yn_done)

            plan = [(copy_acc, "old"), (copy_x3, "gate"), (exp_scores, "attend"),
                    (fourth_q, "linear"), (fourth_k, "linear"), (norm_q, "linear"), (exp_gap, "gate"),
                    (copy_q, "linear"), (copy_gates, "gate"), (norm_h1, "attend"),
                    (copy_x1, "attend"), (norm_y, "old"), (square_qk, "attend"),
                    (copy_qk, "fetch"), (norm_h2, "linear")]

            def body(st):
                for what, stage in plan:
                    if st.at[stage]:
                        what(st.at[stage])

            steps(act, CHUNKS, body)

        @block.vector
        def _(dve):
            dve.wait_ge(x_in, 16)
            nc.vector.tensor_copy(x_f[:], x_s[:]).then_inc(x_f_set, 1)
            nc.vector.memset(emb_t[C:C + 1, :], 1.0).then_inc(emb_t_set, 1)
            dve.wait_ge(x_turned, 1)
            nc.vector.tensor_copy(tok_id[:], bank_d[:, 0:SEQS]).then_inc(tok_set, 1)
            for half in range(2):
                dve.wait_ge(emb_turned, 1 + half)
                nc.vector.tensor_copy(emb_t[0:C, half * 512:(half + 1) * 512],
                                      (bank_a if half == 0 else bank_acc)[0:C, :]).then_inc(emb_t_set, 1)
            dve.wait_ge(small_in, SMALL)
            nc.vector.tensor_reduce(qk_mean[:], qkv_w[:, 0:2 * C].rearrange("p (a c) -> p a c", a=2), AX.X, ALU.add)\
              .then_inc(centred, 1)
            dve.wait_ge(centred, 1)
            nc.vector.tensor_scalar(qk_mean[:], qk_mean[:], 1.0 / C, None, ALU.mult).then_inc(centred, 1)
            dve.wait_ge(centred, 2)
            for i in range(2):
                nc.vector.tensor_scalar(qkv_w[:, i * C:(i + 1) * C], qkv_w[:, i * C:(i + 1) * C],
                                        qk_mean[:, i:i + 1], None, ALU.subtract).then_inc(centred, 1)
            dve.wait_ge(b_turned, 1)
            nc.vector.tensor_copy(wv_t[:], bank_z[0][0:C, 0:C + 1]).then_inc(b1_set, 1)
            nc.vector.tensor_scalar(b1_neg[:], bank_z[0][:, 128:128 + E], -1.0, None, ALU.mult).then_inc(b1_set, 1)
            dve.wait_ge(const_set, N_CONST)
            nc.vector.tensor_copy(b1_diag[:].rearrange("p a b -> p (a b)")[:, 0:E * E:E + 1],
                                  bank_z[0][:, 128:128 + E]).then_inc(b1_set, 1)
            dve.wait_ge(fused, 1)
            nc.vector.tensor_copy(qkv_w[:, 2 * C:3 * C], bank_z[1][0:C + 1, 0:C]).then_inc(fused_set, 1)
            dve.wait_ge(fused, 2)
            nc.vector.tensor_tensor(gate_const[:], bank_z[2][0:E, 0:C], b2_s[:], ALU.add).then_inc(fused_set, 1)
            nc.vector.tensor_copy(ident2_r[:], ident2[:]).then_inc(split, 1)
            dve.wait_ge(w1_in, 32)
            nc.vector.tensor_copy(w1_hi[:], w1_raw[:]).then_inc(split, 1)
            dve.wait_ge(split, 2)
            nc.vector.tensor_tensor(w1_lo[:], w1_raw[:], w1_hi[:].bitcast(F32), ALU.subtract).then_inc(split, 1)

            def ln_stats(i, c, src):
                for s in range(CHUNK):
                    nc.vector.bn_stats(stats[i][:, s, :], src[:, s, :]).then_inc(ln_stat[i], 1)

            def ln_means(i, c):
                dve.wait_ge(ln_stat[i], c.at(2 * CHUNK, CHUNK))
                wait(dve, ln_pool[i], c.before(N_LN))
                fixed(dve)
                for s in range(CHUNK):
                    nc.vector.bn_aggr(mv[i][:, s, :], stats[i][:, s, :]).then_inc(ln_stat[i], 1)

            def expert(c, e):
                dve.wait_ge(z_ready, c.at(E, e + 1))
                if e % (E // PARTS) == 0:
                    dve.wait_ge(spread_in[c.parity][e // (E // PARTS)], 16 * (c.half + 1))
                if e >= RING or c.before(E) is not None:
                    dve.wait_ge(hidden_used, c.at(E, e - RING + 1))
                nc.vector.scalar_tensor_tensor(hidden[e % RING][:], bank_z[e % Z_BANKS][:], b1_neg[:, e:e + 1],
                                               spread[c.parity][:, e * TOK:(e + 1) * TOK],
                                               ALU.max, ALU.mult).then_inc(hidden_ready, 1)

            kv_bank = bank_d[:, 0:PAIRS * (C + 1)]
            pv = bank_a[:, 0:CHUNK * (C + 1)].rearrange("p (s c) -> p s c", s=CHUNK)

            def prob_sums(c):
                dve.wait_ge(pv_done, c.at(1, 1))
                nc.vector.reciprocal(rsum[:], pv[:, :, C]).then_inc(h1_step, 1)

            def attended(c):
                dve.wait_ge(h1_step, c.at(2, 1))
                wait(dve, h1b_done, c.before(1))
                wait(dve, x1_done, c.before(CHUNK))
                nc.vector.tensor_tensor(h1[:], pv[:, :, 0:C], rsum[:].unsqueeze(2).to_broadcast([P, CHUNK, C]),
                                        ALU.mult).then_inc(h1_step, 1)

            def h1_stats(c):
                dve.wait_ge(h1_step, c.at(2, 2))
                ln_stats(0, c, h1)

            def h1_means(c):
                ln_means(0, c)

            def sum_squares(c):
                dve.wait_ge(squared, c.at(2, 2))
                nc.vector.tensor_reduce(sq_sum[:].rearrange("p (a s) -> p s a", a=2),
                                        sq[:].rearrange("p s (a c) -> p s a c", a=2), AX.X, ALU.add).then_inc(q_step, 1)

            def invert_sums(c):
                dve.wait_ge(q_step, c.at(N_Q, 1))
                nc.vector.tensor_scalar(sq_sum[:], sq_sum[:], SUM_EPS, None, ALU.add).then_inc(q_step, 1)
                dve.wait_ge(q_step, c.at(N_Q, 2))
                wait(dve, q_pool, c.before(3))
                nc.vector.reciprocal(sq_rec[:], sq_sum[:]).then_inc(q_step, 1)

            def scale_k(c):
                dve.wait_ge(q_step, c.at(N_Q, 3))
                wait(dve, kv_done, c.before(1))
                nc.vector.tensor_tensor(k2[:], sq[:, :, C:2 * C],
                                        sq_rec[:, CHUNK:2 * CHUNK].unsqueeze(2).to_broadcast([P, CHUNK, C]),
                                        ALU.mult).then_inc(q_step, 1)

            def k_norms(c):
                dve.wait_ge(kv_done, c.at(1, 1))
                wait(dve, k_pool, c.before(1))
                nc.vector.tensor_scalar(k_max[:], kv_bank[:, PAIRS * C:PAIRS * (C + 1)], NORM_EPS ** 2, None, ALU.max)\
                  .then_inc(k_step, 1)

            def norm_kv(c):
                dve.wait_ge(k_pool, c.at(1, 1))
                wait(dve, t2_done, c.before(1))
                nc.vector.scalar_tensor_tensor(kv[:], kv_bank[:, 0:PAIRS * C].rearrange("p (a c) -> p a c", a=PAIRS),
                                               KV_SCALE, k_rn[:].unsqueeze(2).to_broadcast([P, PAIRS, C]),
                                               ALU.mult, ALU.mult).then_inc(k_step, 1)

            def residual(c):
                dve.wait_ge(t2_done, c.at(1, 1))
                dve.wait_ge(h1b_done, c.at(1, 1))
                if not (isinstance(c.number, int) and c.number < 2):
                    dve.wait_ge(h2b_done, c.number - 1)
                for half, bank in ((0, bank_b), (1, bank_c)):
                    v_part = bank[:, 0:2 * 3 * C].rearrange("p (s n) -> p s n", s=2)[:, :, 2 * C:3 * C]
                    nc.vector.tensor_tensor(h2[c.parity][:, 2 * half:2 * half + 2, :], v_part,
                                            h1b[c.parity][:, 2 * half:2 * half + 2, :], ALU.add)\
                      .then_inc(h2_done, 1)

            def h2_stats(c):
                dve.wait_ge(h2_done, c.at(2, 2))
                ln_stats(1, c, h2[c.parity])

            def h2_means(c):
                ln_means(1, c)

            def add_gate_bias(c):
                dve.wait_ge(logits_done, c.at(1, 1))
                nc.vector.tensor_tensor(logits[:], bank_d[:, 0:CHUNK * E].rearrange("p (s e) -> p s e", s=CHUNK),
                                        gate_bias[:].unsqueeze(1).to_broadcast([P, CHUNK, E]), ALU.add)\
                  .then_inc(gate_step, 1)

            def largest(c):
                dve.wait_ge(gate_step, c.at(N_GATE, 1))
                fixed(dve)
                for s in range(CHUNK):
                    nc.vector.max(top[:, s, :], logits[:, s, :]).then_inc(gate_step, 1)

            def places(c):
                dve.wait_ge(gate_step, c.at(N_GATE, 1 + CHUNK))
                fixed(dve)
                for s in range(CHUNK):
                    nc.vector.max_index(top_at[:, s, :], top[:, s, :], logits[:, s, :]).then_inc(gate_step, 1)
                nc.vector.tensor_tensor(gap[:], top[:, :, 1], top[:, :, 0], ALU.subtract).then_inc(gate_step, 1)

            def choose(c):
                dve.wait_ge(gate_step, c.at(N_GATE, 1 + 2 * CHUNK))
                wait(dve, pool_gate, c.before(2))
                nc.vector.tensor_tensor(chosen[:], iota[:].unsqueeze(1).unsqueeze(1).to_broadcast([P, CHUNK, 2, E]),
                                        top_at[:, :, 0:2].unsqueeze(3).to_broadcast([P, CHUNK, 2, E]),
                                        ALU.is_equal).then_inc(gate_step, 1)
                dve.wait_ge(gap_done, c.at(1, 1))
                nc.vector.tensor_scalar(gap_sum[:], gap_exp[:], 1.0, None, ALU.add).then_inc(gate_step, 1)
                dve.wait_ge(gate_step, c.at(N_GATE, 4 + 2 * CHUNK))
                nc.vector.reciprocal(top_w[:, :, 0], gap_sum[:]).then_inc(gate_step, 1)

            def second_weight(c):
                dve.wait_ge(gate_step, c.at(N_GATE, 5 + 2 * CHUNK))
                nc.vector.tensor_tensor(top_w[:, :, 1], gap_exp[:], top_w[:, :, 0], ALU.mult).then_inc(gate_step, 1)

            def add_halves(c):
                dve.wait_ge(acc_turned, c.at(1, 1))
                wait(dve, yn_done, c.before(CHUNK))
                nc.vector.tensor_reduce(y[:], bank_a[:].rearrange("p (s a c) -> p s c a", s=CHUNK, a=2), AX.X, ALU.add)\
                  .then_inc(y_done, 1)

            def y_stats(c):
                dve.wait_ge(y_done, c.at(1, 1))
                ln_stats(2, c, y)

            def y_means(c):
                ln_means(2, c)

            plan = [
                [],
                [(sum_squares, "linear")],
                [(invert_sums, "linear")],
                [(scale_k, "linear")],
                [(prob_sums, "attend"), (add_gate_bias, "gate")],
                [(attended, "attend"), (largest, "gate"), (k_norms, "linear")],
                [(places, "gate")],
                [(norm_kv, "linear"), (h1_stats, "attend"), (choose, "gate")],
                [(second_weight, "gate"), (h1_means, "attend"), (add_halves, "old")],
                [(y_stats, "old")],
                [(y_means, "old")],
                [(residual, "linear")],
                [(h2_stats, "linear")],
                [(h2_means, "linear")],
                [],
                [],
            ]

            def body(st):
                for e in range(E):
                    if st.moe:
                        expert(st.moe, e)
                    for what, stage in plan[e]:
                        if st.at[stage]:
                            what(st.at[stage])

            steps(dve, CHUNKS, body)

        @block.tensor
        def _(pe):
            pe.wait_ge(const_set, N_CONST)
            pe.wait_ge(x_f_set, 1)
            pe.transpose(bank_d[:, 0:SEQS], x_f[:], ident[0:SEQS, 0:SEQS]).then_inc(x_turned, 1)
            pe.wait_ge(emb_in, 16)
            for t in range(VT):
                bank = bank_a if t < VT // 2 else bank_acc
                ins = pe.transpose(bank[0:C, t % (VT // 2) * P:(t % (VT // 2) + 1) * P], emb_s[:, t, :], ident[:])
                if t % (VT // 2) == VT // 2 - 1:
                    ins.then_inc(emb_turned, 1)
            pe.wait_ge(tokw_in, 6 * 16)
            for t in range(VT):
                pe.wait_ge(emb_t_set, 2 + t // (VT // 2))
                if t >= 2:
                    pe.wait_ge(table_ev, t - 1)
                pe.matmul((bank_b if t % 2 == 0 else bank_c)[:, 0:3 * C], emb_t[:, t * P:(t + 1) * P], tok_w[:],
                          start=True, stop=True).then_inc(table_mm, 1)
            pe.wait_ge(small_in, SMALL)
            pe.transpose(bank_z[0][0:C, 0:C + 1], qkv_w[:, 2 * C:3 * C], ident[0:C + 1, 0:C + 1])
            pe.transpose(bank_z[0][:, 128:128 + E], b1_s[:], ident[0:E, 0:E]).then_inc(b_turned, 1)
            pe.wait_ge(b1_set, 3)
            pe.matmul(bank_z[1][0:C + 1, 0:C], wv_t[:], wout[:], start=True, stop=True).then_inc(fused, 1)
            for e in range(E):
                ins = pe.matmul(bank_z[2][0:E, 0:C], b1_diag[:, e, :], w2_s[:, e, :], start=(e == 0), stop=(e == E - 1))
            ins.then_inc(fused, 1)
            pe.wait_ge(fused_set, 2)
            pe.wait_ge(centred, 4)

            def half_of(s):
                return s // PAIRS, s % PAIRS

            order = [0, 2, 1, 3]

            def turn_qk(st):
                c = st.fetch
                if st.attend:
                    pe.wait_ge(x1_copied, st.attend.at(1, 1))
                pe.wait_ge(gathered[c.parity], 64 * (c.half + 1))
                for s in range(CHUNK):
                    ins = pe.transpose(bank_a[:, s * P:(s + 1) * P], gath[c.parity][:, s, 0:2 * C], ident[:])
                ins.then_inc(qk_turned, 1)

            def scores(c):
                pe.wait_ge(qk_copied, c.at(2, 2))
                for s in range(CHUNK):
                    cols = slice(s * P, (s + 1) * P)
                    ins = pe.matmul(bank_a[:, cols], qk_t[:, 1, cols], qk_t[:, 0, cols], start=True, stop=True)
                ins.then_inc(scored, 1)

            def p_v(c):
                pe.wait_ge(exp_done, c.at(1, 1))
                for s in range(CHUNK):
                    ins = pe.matmul(bank_a[:, s * (C + 1):(s + 1) * (C + 1)], probs[:, s, :],
                                    gath[c.parity][:, s, 2 * C:3 * C + 1], start=True, stop=True)
                ins.then_inc(pv_done, 1)

            def turn_acc(st):
                pe.wait_ge(acc_copied, st.old.at(1, 1))
                if st.attend:
                    pe.wait_ge(h1_step, st.attend.at(2, 2))
                for s in range(CHUNK):
                    ins = pe.transpose(bank_a[:, s * P:(s + 1) * P], acc[:, s * P:(s + 1) * P], ident[:])
                ins.then_inc(acc_turned, 1)

            def turn_gates(st):
                pe.wait_ge(pool_gate, st.gate.at(2, 2))
                if st.old:
                    pe.wait_ge(y_done, st.old.at(1, 1))
                elif st.attend:
                    pe.wait_ge(h1_step, st.attend.at(2, 2))
                for s in range(CHUNK):
                    ins = pe.transpose(bank_a[0:E, s * P:(s + 1) * P], gates[:, s, :], ident[:])
                ins.then_inc(gates_turned, 1)

            def turn_x1(st):
                pe.wait_ge(x1_done, st.attend.at(CHUNK, CHUNK))
                if st.gate:
                    pe.wait_ge(gates_copied, st.gate.at(1, 1))
                for s in range(CHUNK):
                    ins = pe.transpose(bank_a[0:C + 1, s * P:(s + 1) * P], x1[:, s, :], ident[:])
                ins.then_inc(x1_turned, 1)

            def q_k_v(st):
                pe.wait_ge(x1_copied, st.attend.at(1, 1))
                if st.linear:
                    pe.wait_ge(h2_done, st.linear.at(2, 2))
                for s in range(CHUNK):
                    half, pair = half_of(s)
                    ins = pe.matmul((bank_b, bank_c)[half][:, pair * 3 * C:(pair + 1) * 3 * C],
                                    x1_t[:, s * P:(s + 1) * P], qkv_w[:], start=(pair == 0), stop=(pair == PAIRS - 1),
                                    skip_group_check=True)
                ins.then_inc(qkv_done, 1)

            def turn_x3(c):
                pe.wait_ge(x3_low, c.at(1, 1))
                for s in range(CHUNK):
                    ins = pe.transpose(bank_d[:, s * P:(s + 1) * P],
                                       x3_parts[:, s, :, :].rearrange("p a c -> p (a c)"), ident[:])
                ins.then_inc(x3_turned, 1)

            def gate_logits(c):
                pe.wait_ge(x3_copied, c.at(1, 1))
                for s in range(CHUNK):
                    ins = pe.matmul(bank_d[:, s * E:(s + 1) * E], x3_t[c.parity][:, s * P:(s + 1) * P].bitcast(F32),
                                    gate_s[:], start=True, stop=True)
                ins.then_inc(logits_done, 1)

            def k_v(st):
                c = st.linear
                pe.wait_ge(v_copied, c.at(2, 2))
                pe.wait_ge(k4_done, c.at(1, 1))
                if st.gate:
                    pe.wait_ge(gate_step, st.gate.at(N_GATE, 1))
                for s in order:
                    half, pair = half_of(s)
                    rows = slice(half * C, (half + 1) * C)
                    pe.matmul(bank_d[rows, pair * C:(pair + 1) * C], k2[:, s, :], v[:, s, :], start=True, stop=True)
                    ins = pe.matmul(bank_d[rows, PAIRS * C + pair:PAIRS * C + pair + 1], k4[:, s, :], ones[:],
                                    start=True, stop=True)
                ins.then_inc(kv_done, 1)

            def turn_q(c):
                pe.wait_ge(q2n_done, c.at(CHUNK, CHUNK))
                pe.wait_ge(k_step, c.at(N_K, N_K))
                for pair in range(PAIRS):
                    ins = pe.transpose(bank_d[:, pair * P:(pair + 1) * P],
                                       q2n[:, pair, :, :].rearrange("p h c -> p (h c)"), ident[:])
                ins.then_inc(q_turned, 1)

            def add_t2(c):
                pe.wait_ge(q_copied, c.at(1, 1))
                for s in order:
                    half, pair = half_of(s)
                    rows = slice(half * C, (half + 1) * C)
                    at = pair * 3 * C + 2 * C
                    ins = pe.matmul((bank_b, bank_c)[half][:, at:at + C], q2n_t[rows, pair, :], kv[rows, pair, :],
                                    start=False, stop=True, skip_group_check=True)
                ins.then_inc(t2_done, 1)

            def hidden_mm(c, e):
                if e >= Z_BANKS:
                    pe.wait_ge(hidden_ready, c.at(E, e - Z_BANKS + 1))
                elif c.before(E) is not None:
                    last = max(n for n in range(E) if n % Z_BANKS == e % Z_BANKS)
                    pe.wait_ge(hidden_ready, c.before(E, last + 1))
                for i, w in enumerate((w1_hi, w1_lo)):
                    ins = pe.matmul(bank_z[e % Z_BANKS][:], w[:, e * F:(e + 1) * F], x3_t[c.parity][:],
                                    start=(i == 0), stop=(i == 1))
                ins.then_inc(z_ready, 1)

            def out_mm(c, j):
                if j == 0:
                    wait(pe, acc_copied, c.before(1))
                    pe.wait_ge(gates_copied, c.at(1, 1))
                    for half in range(2):
                        cols = slice(half * TOK // 2, (half + 1) * TOK // 2)
                        pe.matmul(bank_acc[half * C:(half + 1) * C, cols], gate_const[:], gates_t[c.parity][:, cols],
                                  start=True, stop=False, skip_group_check=True)
                    pe.matmul(bank_acc[0:C, :], ident2_r[:], x3_t[c.parity][:], start=False, stop=False,
                              skip_group_check=True)
                for e in (2 * j, 2 * j + 1):
                    half = e % 2
                    pe.wait_ge(hidden_ready, c.at(E, e + 1))
                    pe.matmul(bank_acc[half * C:(half + 1) * C, :], w2_s[:, e, :], hidden[e % RING][:],
                              start=False, stop=(e >= E - 2), skip_group_check=True).then_inc(hidden_used, 1)

            def of(stage, what):
                return stage, lambda st: what(st.at[stage])

            plan = [
                ([], [of("attend", scores)]),
                ([of("gate", turn_x3)], [of("gate", gate_logits)]),
                ([of("attend", p_v)], [("linear", k_v)]),
                ([], [("old", turn_acc)]),
                ([of("linear", turn_q)], []),
                ([of("linear", add_t2), ("gate", turn_gates)], []),
                ([], [("attend", turn_x1)]),
                ([("attend", q_k_v)], [("fetch", turn_qk)]),
            ]

            def body(st):
                if st.moe and isinstance(st.moe.number, int) and st.moe.number == 0:
                    pe.wait_ge(split, 3)
                for j in range(SLOTS):
                    if st.moe:
                        hidden_mm(st.moe, 2 * j)
                        hidden_mm(st.moe, 2 * j + 1)
                    for n in range(2):
                        if n == 1 and st.moe and j > 0:
                            out_mm(st.moe, j - 1)
                        for stage, what in plan[j][n]:
                            if st.at[stage]:
                                what(st)
                if st.moe:
                    out_mm(st.moe, SLOTS - 1)

            steps(pe, CHUNKS, body)


_INS = ["x", "L0_tok_emb_table", "L0_tok_Wq", "L0_tok_bq", "L0_tok_Wk", "L0_tok_bk", "L0_tok_Wv", "L0_tok_bv",
        "L0_attn_W_qkv", "L0_attn_b_qkv", "L0_attn_W_out", "L0_attn_b_out", "L0_ffn_gate_w", "L0_ffn_gate_b",
        "L0_ffn_w1", "L0_ffn_b1", "L0_ffn_w2", "L0_ffn_b2", "L0_ffn_gamma", "L0_ffn_beta"]


def kernel(**inputs):
    import numpy as np
    import concourse.bacc as bacc
    from concourse import mybir as _mybir
    from concourse.bass_utils import run_bass_kernel_spmd as run

    nc = bacc.Bacc("TRN2", target_bir_lowering=False, num_devices=1)
    arrays, args = {}, []
    for name in _INS:
        a = np.ascontiguousarray(inputs[name])
        arrays[f"in_{name}"] = a
        args.append(nc.dram_tensor(f"in_{name}", a.shape, _mybir.dt.from_np(a.dtype), kind="ExternalInput").ap())
    shape = (*inputs["x"].shape, inputs["L0_tok_emb_table"].shape[1])
    args.append(nc.dram_tensor("out_0", shape, _mybir.dt.float32, kind="ExternalOutput").ap())
    build(nc, *args)
    r = run(nc, [arrays], core_ids=[0])
    return r.results[0]["out_0"]
```

```python
from contextlib import ExitStack

import concourse.bass as bass
from concourse import mybir

F32 = mybir.dt.float32
F32R = mybir.dt.float32r
I32 = mybir.dt.int32
U32 = mybir.dt.uint32
ACT = mybir.ActivationFunctionType
ALU = mybir.AluOpType
AX = mybir.AxisListType

P = 128
CHUNK = 4
PAIRS = CHUNK // 2
SLOTS = 8
Z_BANKS = 3
RING = 4
PARTS = 4
LN_EPS = 1e-5
SUM_EPS = 1e-7
NORM_EPS = 1e-12


class Chunk:

    def __init__(self, number, half, parity):
        self.number, self.half, self.parity = number, half, parity

    def at(self, per_chunk, n):
        return self.number * per_chunk + n

    def before(self, per_chunk, n=None):
        if isinstance(self.number, int) and self.number == 0:
            return None
        return (self.number - 1) * per_chunk + (per_chunk if n is None else n)


class Step:

    def __init__(self, k, chunks, m=None):
        self.k = k if m is None else None

        def chunk(off):
            n = k + off
            if m is not None:
                return Chunk(2 * m + n, m + n // 2, n % 2)
            return Chunk(n, n // 2, n % 2) if 0 <= n < chunks else None

        self.old, self.moe, self.gate, self.linear, self.attend, self.fetch = (chunk(o) for o in range(-1, 5))
        self.at = {"old": self.old, "moe": self.moe, "gate": self.gate, "linear": self.linear,
                   "attend": self.attend, "fetch": self.fetch}


def steps(engine, chunks, body):
    first, last = 2, (chunks - 4) // 2 * 2
    for k in range(-4, first):
        body(Step(k, chunks))
    with engine.Fori(first // 2, last // 2) as m:
        body(Step(0, chunks, m))
        body(Step(1, chunks, m))
    for k in range(last, chunks + 1):
        body(Step(k, chunks))


def wait(engine, semaphore, value):
    if value is not None:
        engine.wait_ge(semaphore, value)


def build(nc, x, emb, Wq, bq, Wk, bk, Wv, bv, W_qkv, b_qkv, W_out, b_out,
          gate_w, gate_b, w1, b1, w2, b2, gamma, beta, out):
    SEQS, T = x.shape
    VOCAB, C = emb.shape
    E, _, F = w1.shape
    CHUNKS = SEQS // CHUNK
    TOK = CHUNK * T
    VT = VOCAB // P
    GW = 200
    assert T == P and F == P and C == 64 and E == 2 * SLOTS and CHUNKS % 2 == 0
    SCORE_SCALE = float(C) ** -0.5
    KV_SCALE = float(T) ** -0.5
    N_CONST = 17

    gates_dram = [nc.dram_tensor(f"gates{i}", (CHUNK * E, P), F32, kind="Internal").ap() for i in range(2)]
    table = nc.dram_tensor("qkv_table", (VOCAB, 3 * C), F32, kind="Internal").ap()

    with ExitStack() as ctx:
        def sb(name, shape, dt=F32):
            return ctx.enter_context(nc.sbuf_tensor(name, shape, dt))

        def ps(name):
            return ctx.enter_context(nc.psum_tensor(name, [P, 512], F32))

        def sem(name):
            return ctx.enter_context(nc.semaphore(name))

        bank_a, bank_b, bank_c, bank_d, bank_acc = (ps(n) for n in ("bank_a", "bank_b", "bank_c", "bank_d", "bank_acc"))
        bank_z = [ps(f"bank_z{i}") for i in range(Z_BANKS)]

        table_banks = [bank_b, bank_c, bank_z[1], bank_z[2]]

        ident = sb("ident", [P, P])
        ident2 = sb("ident2", [P, C])
        iota = sb("iota", [P, E])
        iota_i = sb("iota_i", [P, E], I32)
        ident2_r = sb("ident2_r", [P, C], F32R)
        ones = sb("ones", [P, 1])
        minus_half = sb("minus_half", [P, CHUNK])
        tok_w = sb("tok_w", [C + 1, 3 * C])
        qkv_w = sb("qkv_w", [C + 1, 3 * C])
        wout = sb("wout", [C, C])
        wv_t = sb("wv_t", [C, C + 1])
        qk_mean = sb("qk_mean", [C + 1, 2])
        gate_s = sb("gate_s", [P, E])
        gate_parts = sb("gate_parts", [P, 2 * E], F32R)
        gate_bias = sb("gate_bias", [P, E])
        w1_raw = sb("w1_raw", [P, E * F])
        w1_hi = sb("w1_hi", [P, E * F], F32R)
        w1_lo = sb("w1_lo", [P, E * F], F32R)
        w2_s = sb("w2_s", [P, E, C])
        b1_s = sb("b1_s", [E, F])
        b1_neg = sb("b1_neg", [P, E])
        b1_diag = sb("b1_diag", [P, E, CHUNK * E])
        b2_s = sb("b2_s", [CHUNK * E, C])
        expert_const = sb("expert_const", [CHUNK * E, C])
        own = sb("own", [CHUNK * E, CHUNK])
        gate_const = sb("gate_const", [CHUNK * E, CHUNK, C])
        out_bias = sb("out_bias", [P, C])
        gamma_s = sb("gamma_s", [P, C])
        beta_s = sb("beta_s", [P, C])
        emb_s = sb("emb_s", [P, VT, C])
        emb_t = sb("emb_t", [C + 1, VOCAB])
        table_s = sb("table_s", [P, VT, 3 * C])
        x_s = sb("x_s", [SEQS, T], I32)
        x_f = sb("x_f", [SEQS, T])
        tok_id = sb("tok_id", [P, SEQS], I32)
        rows_now = [sb(f"rows_now{i}", [P, CHUNK], I32) for i in range(2)]
        gath = [sb(f"gath{i}", [P, CHUNK, GW]) for i in range(2)]
        qk_t = sb("qk_t", [C, 2, TOK])
        probs = sb("probs", [P, CHUNK, P])
        rsum = sb("rsum", [P, CHUNK])
        h1 = sb("h1", [P, CHUNK, C])
        h1b = [sb(f"h1b{i}", [P, CHUNK, C]) for i in range(2)]
        x1 = sb("x1", [P, CHUNK, C + 1])
        x1_t = sb("x1_t", [C + 1, TOK])
        sq = sb("sq", [P, CHUNK, 2 * C])
        v = sb("v", [P, CHUNK, C])
        sq_sum = sb("sq_sum", [P, 2 * CHUNK])
        sq_rec = sb("sq_rec", [P, 2 * CHUNK])
        k2 = sb("k2", [P, CHUNK, C])
        k4 = sb("k4", [P, CHUNK, C])
        q4 = sb("q4", [P, CHUNK, C])
        q4_sum = sb("q4_sum", [P, CHUNK])
        q4_max = sb("q4_max", [P, CHUNK])
        q_rn = sb("q_rn", [P, CHUNK])
        q_scale = sb("q_scale", [P, CHUNK])
        q2n = sb("q2n", [P, PAIRS, 2, C])
        q2n_t = sb("q2n_t", [P, PAIRS, P])
        k_max = sb("k_max", [P, PAIRS])
        k_rn = sb("k_rn", [P, PAIRS])
        kv = sb("kv", [P, PAIRS, 2, C])
        h2 = [sb(f"h2{i}", [P, CHUNK, C]) for i in range(2)]
        h2b = [sb(f"h2b{i}", [P, CHUNK, C]) for i in range(2)]
        x3 = sb("x3", [P, CHUNK, C])
        x3_parts = sb("x3_parts", [P, CHUNK, 2, C])
        x3_t = [sb(f"x3_t{i}", [P, TOK], F32R) for i in range(2)]
        logits_low = sb("logits_low", [P, CHUNK, E])
        logits = sb("logits", [P, CHUNK, E])
        top = sb("top", [P, CHUNK, 8])
        top_at = sb("top_at", [P, CHUNK, 8], U32)
        gap = sb("gap", [P, CHUNK])
        gap_exp = sb("gap_exp", [P, CHUNK])
        gap_sum = sb("gap_sum", [P, CHUNK])
        top_w = sb("top_w", [P, CHUNK, 2])
        chosen = sb("chosen", [P, CHUNK, 2, E])
        weighed = sb("weighed", [P, CHUNK, 2, E])
        gates = sb("gates", [P, CHUNK, E])
        gates_t = [sb(f"gates_t{i}", [CHUNK * E, P]) for i in range(2)]
        spread = [sb(f"spread{i}", [P, CHUNK, E, P]) for i in range(2)]
        hidden = [sb(f"hidden{i}", [P, TOK]) for i in range(RING)]
        acc = sb("acc", [P, TOK])
        y = sb("y", [P, CHUNK, C])
        yn = sb("yn", [P, CHUNK, C])
        yg = sb("yg", [P, CHUNK, C])
        res = sb("res", [P, CHUNK, C])
        stats = [sb(f"stats{i}", [P, CHUNK, 6]) for i in range(3)]
        mv = [sb(f"mv{i}", [P, CHUNK, 2]) for i in range(3)]
        var = [sb(f"var{i}", [P, CHUNK]) for i in range(3)]
        neg_mean = [sb(f"neg_mean{i}", [P, CHUNK]) for i in range(3)]
        rstd = [sb(f"rstd{i}", [P, CHUNK]) for i in range(3)]
        shift = [sb(f"shift{i}", [P, CHUNK]) for i in range(3)]

        x_in = sem("x_in")
        emb_in = sem("emb_in")
        tokw_in = sem("tokw_in")
        attn_in = sem("attn_in")
        gate_in = sem("gate_in")
        w2_in = sem("w2_in")
        bias_in = sem("bias_in")
        w1_in = sem("w1_in")
        const_set = sem("const_set")
        x_f_set = sem("x_f_set")
        x_turned = sem("x_turned")
        tok_set = sem("tok_set")
        emb_turned = sem("emb_turned")
        emb_t_set = sem("emb_t_set")
        table_mm = sem("table_mm")
        table_ev = sem("table_ev")
        table_out = sem("table_out")
        centred = sem("centred")
        split = sem("split")
        b_turned = sem("b_turned")
        b1_set = sem("b1_set")
        const_mm = sem("const_mm")
        const_done = sem("const_done")
        fused = sem("fused")
        fused_set = sem("fused_set")
        qk_turned = sem("qk_turned")
        scored = sem("scored")
        pv_done = sem("pv_done")
        x1_turned = sem("x1_turned")
        qkv_done = sem("qkv_done")
        kv_done = sem("kv_done")
        q_turned = sem("q_turned")
        t2_done = sem("t2_done")
        x3_turned = sem("x3_turned")
        logits_done = sem("logits_done")
        gates_turned = sem("gates_turned")
        z_ready = sem("z_ready")
        hidden_used = sem("hidden_used")
        acc_turned = sem("acc_turned")
        qk_copied = sem("qk_copied")
        exp_done = sem("exp_done")
        x1_done = sem("x1_done")
        x1_copied = sem("x1_copied")
        squared = sem("squared")
        v_copied = sem("v_copied")
        q4_done = sem("q4_done")
        k4_done = sem("k4_done")
        q2n_done = sem("q2n_done")
        q_copied = sem("q_copied")
        x3_done = sem("x3_done")
        x3_high = sem("x3_high")
        x3_copied = sem("x3_copied")
        gap_done = sem("gap_done")
        gates_copied = sem("gates_copied")
        acc_copied = sem("acc_copied")
        yn_done = sem("yn_done")
        ln_stat = [sem(f"ln_stat{i}") for i in range(3)]
        h1_step = sem("h1_step")
        q_step = sem("q_step")
        k_step = sem("k_step")
        h2_done = sem("h2_done")
        y_done = sem("y_done")
        gate_step = sem("gate_step")
        hidden_ready = sem("hidden_ready")
        rows_set = sem("rows_set")
        ln_pool = [sem(f"ln_pool{i}") for i in range(3)]
        h1b_done = sem("h1b_done")
        q_pool = sem("q_pool")
        k_pool = sem("k_pool")
        x3_low = sem("x3_low")
        pool_gate = sem("pool_gate")
        h2b_done = sem("h2b_done")
        yg_done = sem("yg_done")
        res_done = sem("res_done")
        gathered = [sem(f"gathered{i}") for i in range(2)]
        gates_out = [sem(f"gates_out{i}") for i in range(2)]
        spread_in = [[sem(f"spread_in{i}_{n}") for n in range(PARTS)] for i in range(2)]
        stored = sem("stored")

        N_Q, N_K, N_LN, N_GATE = 4, 3, 4, 7 + 2 * CHUNK

        def fixed(engine):
            engine.nop(nofuse=True)

        block = ctx.enter_context(nc.Block())

        @block.sync
        def _(sp):
            sp.dma_start(emb_s[:], emb.rearrange("(t p) c -> p t c", p=P)).then_inc(emb_in, 16)
            sp.dma_start(x_s[:], x).then_inc(x_in, 16)
            for i, (w, b) in enumerate(((Wq, bq), (Wk, bk), (Wv, bv))):
                sp.dma_start(tok_w[0:C, i * C:(i + 1) * C], w).then_inc(tokw_in, 16)
                sp.dma_start(tok_w[C:C + 1, i * C:(i + 1) * C], b.rearrange("(a c) -> a c", a=1)).then_inc(tokw_in, 16)
            sp.dma_start(qkv_w[0:C, :], W_qkv).then_inc(attn_in, 16)
            sp.dma_start(qkv_w[C:C + 1, :], b_qkv.rearrange("(a c) -> a c", a=1)).then_inc(attn_in, 16)
            sp.dma_start(wout[:], W_out).then_inc(attn_in, 16)
            sp.dma_start(b1_s[:], b1).then_inc(attn_in, 16)
            for t in range(0, VT, 2):
                sp.wait_ge(table_ev, t + 2)
                sp.dma_start(table[t * P:(t + 2) * P, :].rearrange("(t p) c -> p t c", p=P), table_s[:, t:t + 2, :])\
                  .then_inc(table_out, 16)
            sp.wait_ge(gathered[0], 16 * CHUNK)
            for half in range(2):
                sp.dma_start(w1_raw[half * C:(half + 1) * C, :].rearrange("c (e f) -> c e f", e=E),
                             w1.rearrange("e c f -> c e f")).then_inc(w1_in, 16)
            sp.dma_start(w2_s[:], w2.rearrange("e f c -> f e c")).then_inc(w2_in, 16)
            for half in range(2):
                sp.dma_start(gate_s[half * C:(half + 1) * C, :], gate_w).then_inc(gate_in, 16)
            for s in range(CHUNK):
                sp.dma_start(b2_s[s * E:(s + 1) * E, :], b2).then_inc(w2_in, 16)
            sp.dma_start(out_bias[:], b_out.partition_broadcast(P)).then_inc(bias_in, 16)
            sp.dma_start(gate_bias[:], gate_b.partition_broadcast(P)).then_inc(gate_in, 16)
            sp.dma_start(gamma_s[:], gamma.partition_broadcast(P)).then_inc(bias_in, 16)
            sp.dma_start(beta_s[:], beta.partition_broadcast(P)).then_inc(bias_in, 16)

            def body(st):
                if st.gate:
                    c = st.gate
                    sp.wait_ge(gates_copied, c.at(1, 1))
                    fixed(sp)
                    if not (isinstance(c.number, int) and c.number < 2):
                        sp.wait_ge(hidden_ready, (c.number - 1) * E)
                    sp.dma_start(gates_dram[c.parity], gates_t[c.parity][:]).then_inc(gates_out[c.parity], 16)
                    sp.wait_ge(gates_out[c.parity], 16 * (c.half + 1))
                    n = E // PARTS
                    for i in range(PARTS):
                        rows = gates_dram[c.parity].rearrange("(s e) t -> s e t", s=CHUNK)[:, i * n:(i + 1) * n, :]
                        sp.dma_start(spread[c.parity][:, :, i * n:(i + 1) * n, :], rows.partition_broadcast(P))\
                          .then_inc(spread_in[c.parity][i], 16)
                if st.old:
                    c = st.old
                    sp.wait_ge(res_done, c.at(1, 1))
                    fixed(sp)
                    rows = out[bass.ds(c.number * CHUNK, CHUNK), :, :].rearrange("s t c -> t s c")
                    sp.dma_start(rows, res[:]).then_inc(stored, 16)

            steps(sp, CHUNKS, body)
            sp.wait_ge(stored, 16 * CHUNKS)

        @block.gpsimd
        def _(pool):
            nc.gpsimd.memset(ident[:], 0.0).then_inc(const_set, 1)
            nc.gpsimd.memset(ident2[:], 0.0).then_inc(const_set, 1)
            nc.gpsimd.memset(minus_half[:], -0.5).then_inc(const_set, 1)
            nc.gpsimd.iota(iota_i[:], pattern=[[1, E]], base=0, channel_multiplier=0).then_inc(const_set, 1)
            pool.wait_ge(const_set, 4)
            nc.gpsimd.affine_select(out=ident[:], in_=ident[:], compare_op=ALU.not_equal, fill=1.0, base=0,
                                    pattern=[[-1, P]], channel_multiplier=1).then_inc(const_set, 1)
            nc.gpsimd.affine_select(out=ident2[:], in_=ident2[:], compare_op=ALU.not_equal, fill=1.0, base=0,
                                    pattern=[[-1, C]], channel_multiplier=1).then_inc(const_set, 1)
            pool.wait_ge(const_set, 6)
            nc.gpsimd.affine_select(out=ident2[:], in_=ident2[:], compare_op=ALU.not_equal, fill=1.0, base=-C,
                                    pattern=[[-1, C]], channel_multiplier=1).then_inc(const_set, 1)
            nc.gpsimd.tensor_copy(iota[:], iota_i[:]).then_inc(const_set, 1)
            nc.gpsimd.memset(ones[:], 1.0).then_inc(const_set, 1)
            nc.gpsimd.memset(b1_diag[:], 0.0).then_inc(const_set, 1)
            nc.gpsimd.memset(own[:], 1.0).then_inc(const_set, 1)
            pool.wait_ge(const_set, 11)
            nc.gpsimd.affine_select(out=own[:], in_=own[:], compare_op=ALU.is_ge, fill=0.0, base=0,
                                    pattern=[[-E, CHUNK]], channel_multiplier=1).then_inc(const_set, 1)
            pool.wait_ge(const_set, 12)
            nc.gpsimd.affine_select(out=own[:], in_=own[:], compare_op=ALU.is_ge, fill=0.0, base=E - 1,
                                    pattern=[[E, CHUNK]], channel_multiplier=-1).then_inc(const_set, 1)
            nc.gpsimd.memset(kv[:], 0.0).then_inc(const_set, 1)
            nc.gpsimd.memset(x1[:, :, C:C + 1], 1.0).then_inc(const_set, 1)
            nc.gpsimd.memset(gath[0][:, :, 3 * C:3 * C + 1], 1.0).then_inc(const_set, 1)
            nc.gpsimd.memset(gath[1][:, :, 3 * C:3 * C + 1], 1.0).then_inc(const_set, 1)
            pool.wait_ge(table_out, 16 * VT // 2)
            pool.wait_ge(tok_set, 1)

            def gather(c, first, last):
                if first == 0:
                    if not (isinstance(c.number, int) and c.number < 2):
                        pool.wait_ge(pv_done, c.number - 1)
                        pool.wait_ge(gathered[c.parity], 16 * CHUNK * c.half)
                    nc.gpsimd.tensor_copy(rows_now[c.parity][:], tok_id[:, bass.ds(c.number * CHUNK, CHUNK)])\
                      .then_inc(rows_set, 1)
                    pool.wait_ge(rows_set, c.at(1, 1))
                    fixed(pool)
                for s in range(first, last):
                    nc.gpsimd.indirect_dma_start(
                        gath[c.parity][:, s, 0:3 * C], None, table,
                        bass.IndirectOffsetOnAxis(ap=rows_now[c.parity][:, s:s + 1], axis=0),
                    ).then_inc(gathered[c.parity], 16)

            def ln_factors(i, c):
                pool.wait_ge(ln_stat[i], c.at(2 * CHUNK, 2 * CHUNK))
                fixed(pool)
                nc.gpsimd.tensor_scalar(var[i][:], mv[i][:, :, 1], LN_EPS, None, ALU.add).then_inc(ln_pool[i], 1)
                nc.gpsimd.tensor_scalar(neg_mean[i][:], mv[i][:, :, 0], -1.0, None, ALU.mult).then_inc(ln_pool[i], 1)
                pool.wait_ge(ln_pool[i], c.at(N_LN, 1))
                nc.gpsimd.tensor_tensor(rstd[i][:], var[i][:], minus_half[:], ALU.pow).then_inc(ln_pool[i], 1)
                pool.wait_ge(ln_pool[i], c.at(N_LN, 3))
                nc.gpsimd.tensor_tensor(shift[i][:], neg_mean[i][:], rstd[i][:], ALU.mult).then_inc(ln_pool[i], 1)

            def low_parts(c):
                pool.wait_ge(x3_high, c.at(1, 1))
                wait(pool, x3_turned, c.before(1))
                nc.gpsimd.tensor_tensor(x3_parts[:, :, 1, :], x3[:], x3_parts[:, :, 0, :], ALU.subtract)\
                  .then_inc(x3_low, 1)

            def q_factors(c):
                pool.wait_ge(q4_done, c.at(CHUNK, CHUNK))
                fixed(pool)
                nc.gpsimd.tensor_scalar(q4_max[:], q4_sum[:], NORM_EPS ** 2, None, ALU.max).then_inc(q_pool, 1)
                pool.wait_ge(q_pool, c.at(3, 1))
                nc.gpsimd.tensor_tensor(q_rn[:], q4_max[:], minus_half[:], ALU.pow).then_inc(q_pool, 1)
                pool.wait_ge(q_pool, c.at(3, 2))
                wait(pool, q2n_done, c.before(CHUNK))
                nc.gpsimd.tensor_tensor(q_scale[:], q_rn[:], sq_rec[:, 0:CHUNK], ALU.mult).then_inc(q_pool, 1)

            def k_factors(c):
                pool.wait_ge(k_step, c.at(N_K, 1))
                nc.gpsimd.tensor_tensor(k_rn[:], k_max[:], minus_half[:, 0:PAIRS], ALU.pow).then_inc(k_pool, 1)

            def add_out_bias(c):
                if isinstance(c.number, int) and c.number == 0:
                    pool.wait_ge(bias_in, 3 * 16)
                pool.wait_ge(h1_step, c.at(2, 2))
                if not (isinstance(c.number, int) and c.number < 2):
                    pool.wait_ge(h2_done, 2 * (c.number - 1))
                nc.gpsimd.tensor_tensor(h1b[c.parity][:], h1[:], out_bias[:].unsqueeze(1).to_broadcast([P, CHUNK, C]),
                                        ALU.add).then_inc(h1b_done, 1)

            def add_beta(c):
                pool.wait_ge(h2_done, c.at(2, 2))
                if not (isinstance(c.number, int) and c.number < 2):
                    pool.wait_ge(res_done, c.number - 1)
                nc.gpsimd.tensor_tensor(h2b[c.parity][:], h2[c.parity][:],
                                        beta_s[:].unsqueeze(1).to_broadcast([P, CHUNK, C]),
                                        ALU.add).then_inc(h2b_done, 1)

            def make_gates(c):
                pool.wait_ge(gate_step, c.at(N_GATE, N_GATE))
                nc.gpsimd.tensor_tensor(weighed[:], chosen[:], top_w[:].unsqueeze(3).to_broadcast([P, CHUNK, 2, E]),
                                        ALU.mult).then_inc(pool_gate, 1)
                pool.wait_ge(pool_gate, c.at(2, 1))
                wait(pool, gates_turned, c.before(1))
                nc.gpsimd.tensor_tensor(gates[:], weighed[:, :, 0, :], weighed[:, :, 1, :], ALU.add)\
                  .then_inc(pool_gate, 1)

            def result(c):
                pool.wait_ge(yn_done, c.at(CHUNK, CHUNK))
                nc.gpsimd.tensor_tensor(yg[:], yn[:], gamma_s[:].unsqueeze(1).to_broadcast([P, CHUNK, C]),
                                        ALU.mult).then_inc(yg_done, 1)
                pool.wait_ge(yg_done, c.at(1, 1))
                wait(pool, stored, c.before(16))
                nc.gpsimd.tensor_tensor(res[:], yg[:], h2b[c.parity][:], ALU.add).then_inc(res_done, 1)

            def body(st):
                if st.gate:
                    low_parts(st.gate)
                if st.fetch:
                    gather(st.fetch, 0, 3)
                if st.linear:
                    q_factors(st.linear)
                if st.moe:
                    add_beta(st.moe)
                if st.linear:
                    k_factors(st.linear)
                if st.gate:
                    make_gates(st.gate)
                if st.attend:
                    add_out_bias(st.attend)
                if st.fetch:
                    gather(st.fetch, 3, 4)
                if st.attend:
                    ln_factors(0, st.attend)
                if st.old:
                    ln_factors(2, st.old)
                if st.linear:
                    ln_factors(1, st.linear)
                if st.old:
                    result(st.old)

            steps(pool, CHUNKS, body)

        @block.scalar
        def _(act):
            for t in range(VT):
                act.wait_ge(table_mm, t + 1)
                nc.scalar.copy(table_s[:, t, :], table_banks[t % 4][:, 0:3 * C]).then_inc(table_ev, 1)

            def normalise(i, c, dst, src, done):
                act.wait_ge(ln_pool[i], c.at(N_LN, N_LN))
                for s in range(CHUNK):
                    nc.scalar.activation(dst[:, s, :], src[:, s, :], ACT.Identity, bias=shift[i][:, s:s + 1],
                                         scale=rstd[i][:, s:s + 1]).then_inc(done, 1)

            def copy_acc(c):
                act.wait_ge(hidden_used, c.at(E, E))
                wait(act, acc_turned, c.before(1))
                nc.scalar.copy(acc[:], bank_acc[:]).then_inc(acc_copied, 1)

            def copy_qk(c):
                act.wait_ge(qk_turned, c.at(1, 1))
                wait(act, scored, c.before(1))
                for i in range(2):
                    nc.scalar.copy(qk_t[:, i, :], bank_a[i * C:(i + 1) * C, :]).then_inc(qk_copied, 1)

            def exp_scores(c):
                act.wait_ge(scored, c.at(1, 1))
                wait(act, pv_done, c.before(1))
                nc.scalar.activation(probs[:].rearrange("p s t -> p (s t)"), bank_a[:], ACT.Exp, scale=SCORE_SCALE)\
                  .then_inc(exp_done, 1)

            def norm_h1(c):
                wait(act, x1_turned, c.before(1))
                normalise(0, c, x1[:, :, 0:C], h1, x1_done)

            def copy_x1(c):
                act.wait_ge(x1_turned, c.at(1, 1))
                wait(act, qkv_done, c.before(1))
                nc.scalar.copy(x1_t[:], bank_a[0:C + 1, :]).then_inc(x1_copied, 1)

            def square_qk(c):
                act.wait_ge(qkv_done, c.at(1, 1))
                wait(act, q_step, c.before(N_Q, N_Q))
                wait(act, kv_done, c.before(1))
                for pair, bank in enumerate((bank_b, bank_c)):
                    both = bank[:, 0:2 * 3 * C].rearrange("p (h n) -> p h n", h=2)
                    nc.scalar.activation(sq[:, pair::PAIRS, :], both[:, :, 0:2 * C], ACT.Square).then_inc(squared, 1)
                    nc.scalar.copy(v[:, pair::PAIRS, :], both[:, :, 2 * C:3 * C]).then_inc(v_copied, 1)

            def fourth_q(c):
                act.wait_ge(q_step, c.at(N_Q, 3))
                wait(act, q_pool, c.before(3))
                for s in range(CHUNK):
                    nc.scalar.activation(q4[:, s, :], sq[:, s, 0:C], ACT.Square, scale=sq_rec[:, s:s + 1],
                                         accum_out=q4_sum[:, s:s + 1]).then_inc(q4_done, 1)

            def fourth_k(c):
                act.wait_ge(q_step, c.at(N_Q, 4))
                wait(act, kv_done, c.before(1))
                nc.scalar.activation(k4[:], k2[:], ACT.Square).then_inc(k4_done, 1)

            def norm_q(c):
                act.wait_ge(q_pool, c.at(3, 3))
                wait(act, q_turned, c.before(1))
                for s in range(CHUNK):
                    half, pair = s // PAIRS, s % PAIRS
                    nc.scalar.activation(q2n[:, pair, half, :], sq[:, s, 0:C], ACT.Identity, scale=q_scale[:, s:s + 1])\
                      .then_inc(q2n_done, 1)

            def copy_q(c):
                act.wait_ge(q_turned, c.at(1, 1))
                wait(act, t2_done, c.before(1))
                nc.scalar.copy(q2n_t[:].rearrange("p a t -> p (a t)"), bank_d[:, 0:2 * P]).then_inc(q_copied, 1)

            def norm_h2(c):
                wait(act, x3_low, c.before(1))
                normalise(1, c, x3, h2[c.parity], x3_done)
                act.wait_ge(x3_done, c.at(CHUNK, CHUNK))
                wait(act, x3_turned, c.before(1))
                nc.scalar.copy(x3_parts[:, :, 0, :].bitcast(F32R), x3[:]).then_inc(x3_high, 1)

            def copy_x3(c):
                act.wait_ge(x3_turned, c.at(1, 1))
                if not (isinstance(c.number, int) and c.number < 2):
                    act.wait_ge(hidden_used, (c.number - 1) * E)
                nc.scalar.copy(x3_t[c.parity][:], bank_d[:]).then_inc(x3_copied, 1)

            def exp_gap(c):
                act.wait_ge(gate_step, c.at(N_GATE, 3 + 2 * CHUNK))
                nc.scalar.activation(gap_exp[:], gap[:], ACT.Exp).then_inc(gap_done, 1)

            def copy_gates(c):
                act.wait_ge(gates_turned, c.at(1, 1))
                if not (isinstance(c.number, int) and c.number < 2):
                    act.wait_ge(gates_out[c.parity], 16 * c.half)
                    act.wait_ge(hidden_used, (c.number - 1) * E)
                nc.scalar.copy(gates_t[c.parity][:], bank_d[0:CHUNK * E, 0:P]).then_inc(gates_copied, 1)

            def norm_y(c):
                wait(act, yg_done, c.before(1))
                normalise(2, c, yn, y, yn_done)

            order = [(copy_acc, "old"), (copy_x3, "gate"), (exp_scores, "attend"),
                     (fourth_q, "linear"), (fourth_k, "linear"), (exp_gap, "gate"), (norm_q, "linear"),
                     (copy_q, "linear"), (copy_gates, "gate"), (norm_h1, "attend"),
                     (copy_x1, "attend"), (norm_y, "old"), (square_qk, "attend"),
                     (norm_h2, "linear"), (copy_qk, "fetch")]
            early = order[:-3] + [order[-2], order[-3], order[-1]]

            def body(st):
                for what, stage in early if st.k is not None and st.k < 0 else order:
                    if st.at[stage]:
                        what(st.at[stage])

            steps(act, CHUNKS, body)

        @block.vector
        def _(dve):
            dve.wait_ge(x_in, 16)
            nc.vector.tensor_copy(x_f[:], x_s[:]).then_inc(x_f_set, 1)
            nc.vector.memset(emb_t[C:C + 1, :], 1.0).then_inc(emb_t_set, 1)
            dve.wait_ge(x_turned, 1)
            nc.vector.tensor_copy(tok_id[:], bank_d[:, 0:SEQS]).then_inc(tok_set, 1)
            for half in range(2):
                dve.wait_ge(emb_turned, 1 + half)
                nc.vector.tensor_copy(emb_t[0:C, half * 512:(half + 1) * 512],
                                      (bank_a if half == 0 else bank_acc)[0:C, :]).then_inc(emb_t_set, 1)
            dve.wait_ge(attn_in, 4 * 16)
            nc.vector.tensor_reduce(qk_mean[:], qkv_w[:, 0:2 * C].rearrange("p (a c) -> p a c", a=2), AX.X, ALU.add)\
              .then_inc(centred, 1)
            dve.wait_ge(centred, 1)
            nc.vector.tensor_scalar(qk_mean[:], qk_mean[:], 1.0 / C, None, ALU.mult).then_inc(centred, 1)
            dve.wait_ge(centred, 2)
            for i in range(2):
                nc.vector.tensor_scalar(qkv_w[:, i * C:(i + 1) * C], qkv_w[:, i * C:(i + 1) * C],
                                        qk_mean[:, i:i + 1], None, ALU.subtract).then_inc(centred, 1)
            dve.wait_ge(b_turned, 1)
            nc.vector.tensor_copy(wv_t[:], bank_z[0][0:C, 0:C + 1]).then_inc(b1_set, 1)
            nc.vector.tensor_scalar(b1_neg[:], bank_z[0][:, 128:128 + E], -1.0, None, ALU.mult).then_inc(b1_set, 1)
            dve.wait_ge(const_set, N_CONST)
            for s in range(CHUNK):
                nc.vector.tensor_copy(b1_diag[:].rearrange("p a b -> p (a b)")[:, s * E::CHUNK * E + 1][:, 0:E],
                                      bank_z[0][:, 128:128 + E]).then_inc(b1_set, 1)
            dve.wait_ge(fused, 1)
            nc.vector.tensor_copy(qkv_w[:, 2 * C:3 * C], bank_z[1][0:C + 1, 0:C]).then_inc(fused_set, 1)
            def split_weights():
                nc.vector.tensor_copy(ident2_r[:], ident2[:]).then_inc(split, 1)
                dve.wait_ge(gate_in, 3 * 16)
                nc.vector.tensor_copy(gate_parts[:, 0:E], gate_s[:]).then_inc(split, 1)
                dve.wait_ge(split, 2)
                nc.vector.tensor_tensor(gate_parts[:, E:2 * E], gate_s[:], gate_parts[:, 0:E].bitcast(F32), ALU.subtract)\
                  .then_inc(split, 1)
                dve.wait_ge(w1_in, 32)
                nc.vector.tensor_copy(w1_hi[:], w1_raw[:]).then_inc(split, 1)
                dve.wait_ge(split, 4)
                nc.vector.tensor_tensor(w1_lo[:], w1_raw[:], w1_hi[:].bitcast(F32), ALU.subtract).then_inc(split, 1)

            def ln_stats(i, c, src):
                for s in range(CHUNK):
                    nc.vector.bn_stats(stats[i][:, s, :], src[:, s, :]).then_inc(ln_stat[i], 1)

            def ln_means(i, c):
                dve.wait_ge(ln_stat[i], c.at(2 * CHUNK, CHUNK))
                wait(dve, ln_pool[i], c.before(N_LN))
                fixed(dve)
                for s in range(CHUNK):
                    nc.vector.bn_aggr(mv[i][:, s, :], stats[i][:, s, :]).then_inc(ln_stat[i], 1)

            def expert(c, e):
                dve.wait_ge(z_ready, c.at(E, e + 1))
                if e % (E // PARTS) == 0:
                    dve.wait_ge(spread_in[c.parity][e // (E // PARTS)], 16 * (c.half + 1))
                if e >= RING or c.before(E) is not None:
                    dve.wait_ge(hidden_used, c.at(E, e - RING + 1))
                nc.vector.scalar_tensor_tensor(hidden[e % RING][:].rearrange("p (s t) -> p s t", s=CHUNK),
                                               bank_z[e % Z_BANKS][:].rearrange("p (s t) -> p s t", s=CHUNK),
                                               b1_neg[:, e:e + 1], spread[c.parity][:, :, e, :],
                                               ALU.max, ALU.mult).then_inc(hidden_ready, 1)

            kv_bank = bank_d[:, 0:PAIRS * (C + 1)]
            pv = bank_a[:, 0:CHUNK * (C + 1)].rearrange("p (s c) -> p s c", s=CHUNK)

            def prob_sums(c):
                dve.wait_ge(pv_done, c.at(1, 1))
                nc.vector.reciprocal(rsum[:], pv[:, :, C]).then_inc(h1_step, 1)

            def attended(c):
                dve.wait_ge(h1_step, c.at(2, 1))
                wait(dve, h1b_done, c.before(1))
                wait(dve, x1_done, c.before(CHUNK))
                nc.vector.tensor_tensor(h1[:], pv[:, :, 0:C], rsum[:].unsqueeze(2).to_broadcast([P, CHUNK, C]),
                                        ALU.mult).then_inc(h1_step, 1)

            def h1_stats(c):
                dve.wait_ge(h1_step, c.at(2, 2))
                ln_stats(0, c, h1)

            def h1_means(c):
                ln_means(0, c)

            def sum_squares(c):
                dve.wait_ge(squared, c.at(2, 2))
                nc.vector.tensor_reduce(sq_sum[:].rearrange("p (a s) -> p s a", a=2),
                                        sq[:].rearrange("p s (a c) -> p s a c", a=2), AX.X, ALU.add).then_inc(q_step, 1)

            def invert_sums(c):
                dve.wait_ge(q_step, c.at(N_Q, 1))
                nc.vector.tensor_scalar(sq_sum[:], sq_sum[:], SUM_EPS, None, ALU.add).then_inc(q_step, 1)
                dve.wait_ge(q_step, c.at(N_Q, 2))
                wait(dve, q_pool, c.before(3))
                nc.vector.reciprocal(sq_rec[:], sq_sum[:]).then_inc(q_step, 1)

            def scale_k(c):
                dve.wait_ge(q_step, c.at(N_Q, 3))
                wait(dve, kv_done, c.before(1))
                nc.vector.tensor_tensor(k2[:], sq[:, :, C:2 * C],
                                        sq_rec[:, CHUNK:2 * CHUNK].unsqueeze(2).to_broadcast([P, CHUNK, C]),
                                        ALU.mult).then_inc(q_step, 1)

            def k_norms(c):
                dve.wait_ge(kv_done, c.at(1, 1))
                wait(dve, k_pool, c.before(1))
                nc.vector.tensor_scalar(k_max[:], kv_bank[:, PAIRS * C:PAIRS * (C + 1)], NORM_EPS ** 2, None, ALU.max)\
                  .then_inc(k_step, 1)

            def norm_kv(c):
                dve.wait_ge(k_pool, c.at(1, 1))
                wait(dve, t2_done, c.before(1))
                for half in range(2):
                    rows = slice(half * C, (half + 1) * C)
                    nc.vector.scalar_tensor_tensor(kv[rows, :, half, :],
                                                   kv_bank[rows, 0:PAIRS * C].rearrange("p (a c) -> p a c", a=PAIRS),
                                                   KV_SCALE, k_rn[rows, :].unsqueeze(2).to_broadcast([C, PAIRS, C]),
                                                   ALU.mult, ALU.mult).then_inc(k_step, 1)

            def residual(c):
                dve.wait_ge(t2_done, c.at(1, 1))
                dve.wait_ge(h1b_done, c.at(1, 1))
                if not (isinstance(c.number, int) and c.number < 2):
                    dve.wait_ge(h2b_done, c.number - 1)
                for pair, bank in enumerate((bank_b, bank_c)):
                    v_part = bank[:, 0:2 * 3 * C].rearrange("p (h n) -> p h n", h=2)[:, :, 2 * C:3 * C]
                    nc.vector.tensor_tensor(h2[c.parity][:, pair::PAIRS, :], v_part,
                                            h1b[c.parity][:, pair::PAIRS, :], ALU.add)\
                      .then_inc(h2_done, 1)

            def h2_stats(c):
                dve.wait_ge(h2_done, c.at(2, 2))
                ln_stats(1, c, h2[c.parity])

            def h2_means(c):
                ln_means(1, c)

            logit_parts = bank_d[:, 0:CHUNK * 2 * E].rearrange("p (s a e) -> p s a e", s=CHUNK, a=2)

            def add_gate_bias(c):
                dve.wait_ge(logits_done, c.at(1, 1))
                nc.vector.tensor_tensor(logits_low[:], logit_parts[:, :, 1, :],
                                        gate_bias[:].unsqueeze(1).to_broadcast([P, CHUNK, E]), ALU.add)\
                  .then_inc(gate_step, 1)

            def add_parts(c):
                dve.wait_ge(gate_step, c.at(N_GATE, 1))
                nc.vector.tensor_tensor(logits[:], logit_parts[:, :, 0, :], logits_low[:], ALU.add)\
                  .then_inc(gate_step, 1)

            def largest(c):
                dve.wait_ge(gate_step, c.at(N_GATE, 2))
                fixed(dve)
                for s in range(CHUNK):
                    nc.vector.max(top[:, s, :], logits[:, s, :]).then_inc(gate_step, 1)

            def places(c):
                dve.wait_ge(gate_step, c.at(N_GATE, 2 + CHUNK))
                fixed(dve)
                for s in range(CHUNK):
                    nc.vector.max_index(top_at[:, s, :], top[:, s, :], logits[:, s, :]).then_inc(gate_step, 1)
                nc.vector.tensor_tensor(gap[:], top[:, :, 1], top[:, :, 0], ALU.subtract).then_inc(gate_step, 1)

            def choose(c):
                dve.wait_ge(gate_step, c.at(N_GATE, 2 + 2 * CHUNK))
                wait(dve, pool_gate, c.before(2))
                nc.vector.tensor_tensor(chosen[:], iota[:].unsqueeze(1).unsqueeze(1).to_broadcast([P, CHUNK, 2, E]),
                                        top_at[:, :, 0:2].unsqueeze(3).to_broadcast([P, CHUNK, 2, E]),
                                        ALU.is_equal).then_inc(gate_step, 1)
                dve.wait_ge(gap_done, c.at(1, 1))
                nc.vector.tensor_scalar(gap_sum[:], gap_exp[:], 1.0, None, ALU.add).then_inc(gate_step, 1)
                dve.wait_ge(gate_step, c.at(N_GATE, 5 + 2 * CHUNK))
                nc.vector.reciprocal(top_w[:, :, 0], gap_sum[:]).then_inc(gate_step, 1)

            def second_weight(c):
                dve.wait_ge(gate_step, c.at(N_GATE, 6 + 2 * CHUNK))
                nc.vector.tensor_tensor(top_w[:, :, 1], gap_exp[:], top_w[:, :, 0], ALU.mult).then_inc(gate_step, 1)

            def add_halves(c):
                dve.wait_ge(acc_turned, c.at(1, 1))
                wait(dve, yn_done, c.before(CHUNK))
                nc.vector.tensor_reduce(y[:], bank_a[:].rearrange("p (s a c) -> p s c a", s=CHUNK, a=2), AX.X, ALU.add)\
                  .then_inc(y_done, 1)

            def y_stats(c):
                dve.wait_ge(y_done, c.at(1, 1))
                ln_stats(2, c, y)

            def y_means(c):
                ln_means(2, c)

            plan = [
                [],
                [(sum_squares, "linear")],
                [(invert_sums, "linear")],
                [(scale_k, "linear"), (add_gate_bias, "gate"), (add_parts, "gate"), (largest, "gate")],
                [(places, "gate"), (prob_sums, "attend")],
                [(attended, "attend"), (k_norms, "linear"), (choose, "gate")],
                [(second_weight, "gate"), (norm_kv, "linear")],
                [(h1_stats, "attend")],
                [(h1_means, "attend"), (add_halves, "old")],
                [(y_stats, "old")],
                [(residual, "linear")],
                [(y_means, "old"), (h2_stats, "linear")],
                [(h2_means, "linear")],
                [],
                [],
                [],
            ]

            def body(st):
                if st.k == -2:
                    split_weights()
                    dve.wait_ge(w2_in, (1 + CHUNK) * 16)
                    dve.wait_ge(const_mm, 1)
                    nc.vector.tensor_tensor(expert_const[:], bank_z[2][0:CHUNK * E, 0:C], b2_s[:], ALU.add)\
                      .then_inc(const_done, 1)
                    dve.wait_ge(const_done, 1)
                    nc.vector.tensor_tensor(gate_const[:], expert_const[:].unsqueeze(1).to_broadcast([CHUNK * E, CHUNK, C]),
                                            own[:].unsqueeze(2).to_broadcast([CHUNK * E, CHUNK, C]), ALU.mult)\
                      .then_inc(const_done, 1)
                for e in range(E):
                    if st.moe:
                        expert(st.moe, e)
                    for what, stage in plan[e]:
                        if st.at[stage]:
                            what(st.at[stage])

            steps(dve, CHUNKS, body)

        @block.tensor
        def _(pe):
            pe.wait_ge(const_set, N_CONST)
            pe.wait_ge(x_f_set, 1)
            pe.transpose(bank_d[:, 0:SEQS], x_f[:], ident[0:SEQS, 0:SEQS]).then_inc(x_turned, 1)
            pe.wait_ge(emb_in, 16)
            for t in range(VT):
                bank = bank_a if t < VT // 2 else bank_acc
                ins = pe.transpose(bank[0:C, t % (VT // 2) * P:(t % (VT // 2) + 1) * P], emb_s[:, t, :], ident[:])
                if t % (VT // 2) == VT // 2 - 1:
                    ins.then_inc(emb_turned, 1)
            pe.wait_ge(tokw_in, 6 * 16)
            for t in range(VT):
                pe.wait_ge(emb_t_set, 2 + t // (VT // 2))
                if t >= 4:
                    pe.wait_ge(table_ev, t - 3)
                pe.matmul(table_banks[t % 4][:, 0:3 * C], emb_t[:, t * P:(t + 1) * P], tok_w[:],
                          start=True, stop=True).then_inc(table_mm, 1)
            pe.wait_ge(attn_in, 4 * 16)
            pe.wait_ge(table_ev, VT)
            pe.transpose(bank_z[0][0:C, 0:C + 1], qkv_w[:, 2 * C:3 * C], ident[0:C + 1, 0:C + 1])
            pe.transpose(bank_z[0][:, 128:128 + E], b1_s[:], ident[0:E, 0:E]).then_inc(b_turned, 1)
            pe.wait_ge(b1_set, 2 + CHUNK)
            pe.matmul(bank_z[1][0:C + 1, 0:C], wv_t[:], wout[:], start=True, stop=True).then_inc(fused, 1)
            pe.wait_ge(fused_set, 1)
            pe.wait_ge(centred, 4)

            def half_of(s):
                return s // PAIRS, s % PAIRS

            order = [0, 2, 1, 3]

            def turn_qk(st):
                c = st.fetch
                if st.attend:
                    pe.wait_ge(x1_copied, st.attend.at(1, 1))
                pe.wait_ge(gathered[c.parity], 64 * (c.half + 1))
                for s in range(CHUNK):
                    ins = pe.transpose(bank_a[:, s * P:(s + 1) * P], gath[c.parity][:, s, 0:2 * C], ident[:])
                ins.then_inc(qk_turned, 1)

            def scores(c):
                pe.wait_ge(qk_copied, c.at(2, 2))
                for s in range(CHUNK):
                    cols = slice(s * P, (s + 1) * P)
                    ins = pe.matmul(bank_a[:, cols], qk_t[:, 1, cols], qk_t[:, 0, cols], start=True, stop=True)
                ins.then_inc(scored, 1)

            def p_v(c):
                pe.wait_ge(exp_done, c.at(1, 1))
                for s in range(CHUNK):
                    ins = pe.matmul(bank_a[:, s * (C + 1):(s + 1) * (C + 1)], probs[:, s, :],
                                    gath[c.parity][:, s, 2 * C:3 * C + 1], start=True, stop=True)
                ins.then_inc(pv_done, 1)

            def turn_acc(st):
                pe.wait_ge(acc_copied, st.old.at(1, 1))
                if st.attend:
                    pe.wait_ge(h1_step, st.attend.at(2, 2))
                for s in range(CHUNK):
                    ins = pe.transpose(bank_a[:, s * P:(s + 1) * P], acc[:, s * P:(s + 1) * P], ident[:])
                ins.then_inc(acc_turned, 1)

            def turn_gates(st):
                pe.wait_ge(pool_gate, st.gate.at(2, 2))
                if st.linear:
                    pe.wait_ge(q_copied, st.linear.at(1, 1))
                fixed(pe)
                pe.transpose(bank_d[0:CHUNK * E, 0:P], gates[:].rearrange("p s e -> p (s e)"), ident[:])\
                  .then_inc(gates_turned, 1)

            def turn_x1(st):
                pe.wait_ge(x1_done, st.attend.at(CHUNK, CHUNK))
                if st.old:
                    pe.wait_ge(y_done, st.old.at(1, 1))
                for s in range(CHUNK):
                    ins = pe.transpose(bank_a[0:C + 1, s * P:(s + 1) * P], x1[:, s, :], ident[:])
                ins.then_inc(x1_turned, 1)

            def q_k_v(st):
                pe.wait_ge(x1_copied, st.attend.at(1, 1))
                if st.linear:
                    pe.wait_ge(h2_done, st.linear.at(2, 2))
                for s in range(CHUNK):
                    half, pair = half_of(s)
                    ins = pe.matmul((bank_b, bank_c)[pair][:, half * 3 * C:(half + 1) * 3 * C],
                                    x1_t[:, s * P:(s + 1) * P], qkv_w[:], start=(half == 0), stop=(half == 1),
                                    skip_group_check=True)
                ins.then_inc(qkv_done, 1)

            def turn_x3(st):
                c = st.gate
                pe.wait_ge(x3_low, c.at(1, 1))
                wait(pe, gates_copied, c.before(1))
                for s in range(CHUNK):
                    ins = pe.transpose(bank_d[:, s * P:(s + 1) * P],
                                       x3_parts[:, s, :, :].rearrange("p a c -> p (a c)"), ident[:])
                ins.then_inc(x3_turned, 1)

            def gate_logits(c):
                pe.wait_ge(x3_copied, c.at(1, 1))
                for s in range(CHUNK):
                    ins = pe.matmul(bank_d[:, s * 2 * E:(s + 1) * 2 * E], x3_t[c.parity][:, s * P:(s + 1) * P],
                                    gate_parts[:], start=True, stop=True)
                ins.then_inc(logits_done, 1)

            def k_v(st):
                c = st.linear
                pe.wait_ge(v_copied, c.at(2, 2))
                pe.wait_ge(k4_done, c.at(1, 1))
                if st.gate:
                    pe.wait_ge(gate_step, st.gate.at(N_GATE, 2))
                for s in order:
                    half, pair = half_of(s)
                    rows = slice(half * C, (half + 1) * C)
                    pe.matmul(bank_d[rows, pair * C:(pair + 1) * C], k2[:, s, :], v[:, s, :], start=True, stop=True)
                    ins = pe.matmul(bank_d[rows, PAIRS * C + pair:PAIRS * C + pair + 1], k4[:, s, :], ones[:],
                                    start=True, stop=True)
                ins.then_inc(kv_done, 1)

            def turn_q(c):
                pe.wait_ge(q2n_done, c.at(CHUNK, CHUNK))
                pe.wait_ge(k_step, c.at(N_K, N_K))
                for pair in range(PAIRS):
                    ins = pe.transpose(bank_d[:, pair * P:(pair + 1) * P],
                                       q2n[:, pair, :, :].rearrange("p h c -> p (h c)"), ident[:])
                ins.then_inc(q_turned, 1)

            def add_t2(c):
                pe.wait_ge(q_copied, c.at(1, 1))
                for pair, bank in enumerate((bank_b, bank_c)):
                    v_part = bank[:, 0:2 * 3 * C].rearrange("p (h n) -> p h n", h=2)[:, :, 2 * C:3 * C]
                    ins = pe.matmul(v_part, q2n_t[:, pair, :], kv[:, pair], start=False, stop=True,
                                    skip_group_check=True)
                ins.then_inc(t2_done, 1)

            def hidden_mm(c, e):
                if e >= Z_BANKS:
                    pe.wait_ge(hidden_ready, c.at(E, e - Z_BANKS + 1))
                elif c.before(E) is not None:
                    last = max(n for n in range(E) if n % Z_BANKS == e % Z_BANKS)
                    pe.wait_ge(hidden_ready, c.before(E, last + 1))
                for i, w in enumerate((w1_hi, w1_lo)):
                    ins = pe.matmul(bank_z[e % Z_BANKS][:], w[:, e * F:(e + 1) * F], x3_t[c.parity][:],
                                    start=(i == 0), stop=(i == 1))
                ins.then_inc(z_ready, 1)

            def start_sums(c):
                wait(pe, acc_copied, c.before(1))
                pe.wait_ge(gates_copied, c.at(1, 1))
                fixed(pe)
                for s in order:
                    half, pair = half_of(s)
                    pe.matmul(bank_acc[half * C:(half + 1) * C, s * P:(s + 1) * P], gate_const[:, s, :],
                              gates_t[c.parity][:], start=(pair == 0), stop=False, skip_group_check=True)
                pe.matmul(bank_acc[0:C, :], ident2_r[:], x3_t[c.parity][:], start=False, stop=False,
                          skip_group_check=True)

            def out_mm(c, j):
                for e in (2 * j, 2 * j + 1):
                    half = e % 2
                    pe.wait_ge(hidden_ready, c.at(E, e + 1))
                    pe.matmul(bank_acc[half * C:(half + 1) * C, :], w2_s[:, e, :], hidden[e % RING][:],
                              start=False, stop=(e >= E - 2), skip_group_check=True).then_inc(hidden_used, 1)

            def of(stage, what):
                return stage, lambda st: what(st.at[stage])

            plan = [
                ([], []),
                ([("gate", turn_x3), of("attend", scores), of("moe", start_sums), of("gate", gate_logits)], []),
                ([of("attend", p_v), ("linear", k_v)], []),
                ([], [("old", turn_acc), of("linear", turn_q)]),
                ([("gate", turn_gates)], []),
                ([of("linear", add_t2)], []),
                ([], [("attend", turn_x1)]),
                ([("attend", q_k_v)], [("fetch", turn_qk)]),
            ]

            def body(st):
                if st.k == -1:
                    pe.wait_ge(split, 5)
                    pe.wait_ge(const_done, 2)
                for j in range(SLOTS):
                    if st.k == -3 and j == 3:
                        pe.wait_ge(w2_in, (1 + CHUNK) * 16)
                        for e in range(E):
                            ins = pe.matmul(bank_z[2][0:CHUNK * E, 0:C], b1_diag[:, e, :], w2_s[:, e, :], start=(e == 0),
                                            stop=(e == E - 1))
                        ins.then_inc(const_mm, 1)
                    if st.moe:
                        hidden_mm(st.moe, 2 * j)
                        hidden_mm(st.moe, 2 * j + 1)
                    for n in range(2):
                        if n == 1 and j == 0 and st.old:
                            out_mm(st.old, SLOTS - 1)
                        elif n == 1 and j > 0 and st.moe:
                            out_mm(st.moe, j - 1)
                        for stage, what in plan[j][n]:
                            if st.at[stage]:
                                what(st)

            steps(pe, CHUNKS, body)


_INS = ["x", "L0_tok_emb_table", "L0_tok_Wq", "L0_tok_bq", "L0_tok_Wk", "L0_tok_bk", "L0_tok_Wv", "L0_tok_bv",
        "L0_attn_W_qkv", "L0_attn_b_qkv", "L0_attn_W_out", "L0_attn_b_out", "L0_ffn_gate_w", "L0_ffn_gate_b",
        "L0_ffn_w1", "L0_ffn_b1", "L0_ffn_w2", "L0_ffn_b2", "L0_ffn_gamma", "L0_ffn_beta"]


def kernel(**inputs):
    import numpy as np
    import concourse.bacc as bacc
    from concourse import mybir as _mybir
    from concourse.bass_utils import run_bass_kernel_spmd as run

    nc = bacc.Bacc("TRN2", target_bir_lowering=False, num_devices=1)
    arrays, args = {}, []
    for name in _INS:
        a = np.ascontiguousarray(inputs[name])
        arrays[f"in_{name}"] = a
        args.append(nc.dram_tensor(f"in_{name}", a.shape, _mybir.dt.from_np(a.dtype), kind="ExternalInput").ap())
    shape = (*inputs["x"].shape, inputs["L0_tok_emb_table"].shape[1])
    args.append(nc.dram_tensor("out_0", shape, _mybir.dt.float32, kind="ExternalOutput").ap())
    build(nc, *args)
    r = run(nc, [arrays], core_ids=[0])
    return r.results[0]["out_0"]
```
